# Optimizing a Trainium2 kernel written in Bass

```python
import numpy as np
import jax
import jax.numpy as jnp

def _softmax(x, axis=-1):
    return jax.nn.softmax(x, axis=axis)

def _gelu(x):
    return jax.nn.gelu(x, approximate=True)

def _silu(x):
    return jax.nn.silu(x)

def _sigmoid(x):
    return jax.nn.sigmoid(x)

def _layernorm(x, axis=-1, eps=1e-05):
    m = jnp.mean(x, axis=axis, keepdims=True)
    v = jnp.var(x, axis=axis, keepdims=True)
    return (x - m) / jnp.sqrt(v + eps)

def _scatter_add(tgt, idx, src, axis=0):
    return tgt.at[idx].add(src)

def _segment_sum(src, seg, n):
    return jax.ops.segment_sum(src, seg, n)
kernel_name = 'mk_adaln_d2_jaxref_r4_12a803'

def setup_inputs(seed: int=0):
    np.random.seed(seed)
    _w = jnp.asarray

    def _L0_attn_setup():
        import math
        import jax, jax.numpy as jnp
        import numpy as np
        D_MODEL = 256
        NUM_HEADS = 16
        D_HEAD = D_MODEL // NUM_HEADS
        K_S = 32
        B, N = (2, 512)

        def _attn(x, Wq, bq, Wk, bk, Wv, bv, Wo, bo):
            b, n, _ = x.shape
            q = (x @ Wq.T + bq).reshape(b, n, NUM_HEADS, D_HEAD).transpose(0, 2, 1, 3)
            k = (x @ Wk.T + bk).reshape(b, n, NUM_HEADS, D_HEAD).transpose(0, 2, 1, 3)
            v = (x @ Wv.T + bv).reshape(b, n, NUM_HEADS, D_HEAD).transpose(0, 2, 1, 3)
            scores = jnp.einsum('bhqd,bhkd->bhqk', q, k) / math.sqrt(D_HEAD)
            causal = jnp.triu(jnp.ones((n, n), dtype=bool), k=1)
            neg_inf = jnp.array(-jnp.inf, dtype=scores.dtype)
            scores = jnp.where(causal, neg_inf, scores)
            vals, idx = jax.lax.top_k(scores, K_S)
            masked = jnp.full_like(scores, -jnp.inf)
            masked = jnp.put_along_axis(masked, idx, vals, axis=-1, inplace=False)
            attn = jax.nn.softmax(masked, axis=-1)
            out = jnp.einsum('bhqk,bhkd->bhqd', attn, v)
            out = out.transpose(0, 2, 1, 3).reshape(b, n, D_MODEL)
            y = out @ Wo.T + bo
            return (y, attn.mean(axis=1))

        def _reference_tuple_inner(x, Wq, bq, Wk, bk, Wv, bv, Wo, bo):
            return _attn(x, Wq, bq, Wk, bk, Wv, bv, Wo, bo)
        key = jax.random.key(seed)
        ks = jax.random.split(key, 9)
        s = 1.0 / math.sqrt(D_MODEL)
        return {'x': jax.random.normal(ks[0], (B, N, D_MODEL), dtype=jnp.float32), 'Wq': jax.random.normal(ks[1], (D_MODEL, D_MODEL), dtype=jnp.float32) * s, 'bq': jnp.zeros((D_MODEL,), dtype=jnp.float32), 'Wk': jax.random.normal(ks[2], (D_MODEL, D_MODEL), dtype=jnp.float32) * s, 'bk': jnp.zeros((D_MODEL,), dtype=jnp.float32), 'Wv': jax.random.normal(ks[3], (D_MODEL, D_MODEL), dtype=jnp.float32) * s, 'bv': jnp.zeros((D_MODEL,), dtype=jnp.float32), 'Wo': jax.random.normal(ks[4], (D_MODEL, D_MODEL), dtype=jnp.float32) * s, 'bo': jnp.zeros((D_MODEL,), dtype=jnp.float32)}
    _L0_attn_in = _L0_attn_setup()

    def _L0_ffn_setup():
        import jax, jax.numpy as jnp
        import numpy as np
        B, S, D, E = (4, 1024, 256, 8)
        key = jax.random.key(seed)
        k1, k2, k3, k4, k5 = jax.random.split(key, 5)
        scale = 1.0 / np.sqrt(D)
        return {'x': jax.random.normal(k1, (B, S, D), dtype=jnp.float32), 'Wg': jax.random.normal(k2, (D, D), dtype=jnp.float32) * scale, 'bg': jnp.zeros((D,), dtype=jnp.float32), 'We': jax.random.normal(k3, (E, D, D), dtype=jnp.float32) * scale, 'be': jnp.zeros((E, D), dtype=jnp.float32)}
    _L0_ffn_in = _L0_ffn_setup()
    _L0_c = _w((lambda *s: np.random.randn(*s).astype(np.float32) * 0.05)(4, 256))
    _L0_wmod = _w((lambda *s: np.random.randn(*s).astype(np.float32) * 0.05)(256, 6 * 256) * 256 ** (-0.5))

    def _L1_attn_setup():
        import jax, jax.numpy as jnp
        import numpy as np
        HIDDEN = 256
        NUM_HEADS = 16
        HEAD_SIZE = 64
        key = jax.random.key(seed)
        ks = jax.random.split(key, 5)
        B, S = (2, 512)
        scale = 1.0 / np.sqrt(HIDDEN)
        x = jax.random.normal(ks[0], (B, S, HIDDEN), dtype=jnp.float32)
        W_qkv = jax.random.normal(ks[1], (HIDDEN, 3 * NUM_HEADS * HEAD_SIZE), dtype=jnp.float32) * scale
        b_qkv = jnp.zeros((3 * NUM_HEADS * HEAD_SIZE,), dtype=jnp.float32)
        W_out = jax.random.normal(ks[2], (NUM_HEADS * HEAD_SIZE, HIDDEN), dtype=jnp.float32) * scale
        b_out = jnp.zeros((HIDDEN,), dtype=jnp.float32)
        return {'x': x, 'W_qkv': W_qkv, 'b_qkv': b_qkv, 'W_out': W_out, 'b_out': b_out}
    _L1_attn_in = _L1_attn_setup()

    def _L1_ffn_setup():
        import jax, jax.numpy as jnp
        import numpy as np
        B, T, C, H, E, K, F = (2, 512, 256, 16, 8, 2, 512)
        EPS = 1e-05

        def layernorm(x, w):
            m = x.mean(-1, keepdims=True)
            v = x.var(-1, keepdims=True)
            return (x - m) * jax.lax.rsqrt(v + EPS) * w

        def attention(x, c_attn_w, c_proj_w):
            b, t, c = x.shape
            hd = c // H
            q, k, v = jnp.split(x @ c_attn_w, 3, axis=-1)
            q = q.reshape(b, t, H, hd).transpose(0, 2, 1, 3)
            k = k.reshape(b, t, H, hd).transpose(0, 2, 1, 3)
            v = v.reshape(b, t, H, hd).transpose(0, 2, 1, 3)
            att = jnp.einsum('bhqd,bhkd->bhqk', q, k) / jnp.sqrt(jnp.asarray(hd, x.dtype))
            causal = jnp.tril(jnp.ones((t, t), bool))
            att = jnp.where(causal, att, jnp.asarray(-jnp.inf, att.dtype))
            att = jax.nn.softmax(att, axis=-1)
            y = jnp.einsum('bhqk,bhkd->bhqd', att, v)
            y = y.transpose(0, 2, 1, 3).reshape(b, t, c)
            return y @ c_proj_w

        def moe_mlp(x, router_w, w1, w2):
            b, t, c = x.shape
            xf = x.reshape(-1, c)
            router_logits = xf @ router_w
            probs = jax.nn.softmax(router_logits.astype(jnp.float32), axis=-1)
            rw, sel = jax.lax.top_k(probs, K)
            rw = rw / rw.sum(axis=-1, keepdims=True)
            rw = rw.astype(x.dtype)
            w1e = w1.reshape(c, E, F).transpose(1, 0, 2)
            w2e = w2.reshape(E, F, c)
            h = jax.nn.gelu(jnp.einsum('nc,ecf->enf', xf, w1e), approximate=False)
            y_all = jnp.einsum('enf,efc->nec', h, w2e)
            y_sel = jnp.take_along_axis(y_all, sel[:, :, None], axis=1)
            y = (y_sel * rw[:, :, None]).sum(axis=1)
            return y.reshape(b, t, c)
        key = jax.random.key(seed)
        ks = jax.random.split(key, 6)
        s = 0.02
        return {'x': jax.random.normal(ks[0], (B, T, C), jnp.float32), 'ln1_w': jnp.ones((C,), jnp.float32), 'c_attn_w': jax.random.normal(ks[1], (C, 3 * C), jnp.float32) * s, 'c_proj_w': jax.random.normal(ks[2], (C, C), jnp.float32) * s, 'ln2_w': jnp.ones((C,), jnp.float32), 'router_w': jax.random.normal(ks[3], (C, E), jnp.float32) * s, 'w1': jnp.clip(jax.random.normal(ks[4], (C, E * F), jnp.float32) * s, -0.06, 0.06), 'w2': jnp.clip(jax.random.normal(ks[5], (E * F, C), jnp.float32) * s, -0.06, 0.06)}
    _L1_ffn_in = _L1_ffn_setup()
    _L1_c = _w((lambda *s: np.random.randn(*s).astype(np.float32) * 0.05)(4, 256))
    _L1_wmod = _w((lambda *s: np.random.randn(*s).astype(np.float32) * 0.05)(256, 6 * 256) * 256 ** (-0.5))
    _d = {'L0_attn_x': _L0_attn_in['x'], 'L0_attn_Wq': _L0_attn_in['Wq'], 'L0_attn_bq': _L0_attn_in['bq'], 'L0_attn_Wk': _L0_attn_in['Wk'], 'L0_attn_bk': _L0_attn_in['bk'], 'L0_attn_Wv': _L0_attn_in['Wv'], 'L0_attn_bv': _L0_attn_in['bv'], 'L0_attn_Wo': _L0_attn_in['Wo'], 'L0_attn_bo': _L0_attn_in['bo'], 'L0_ffn_Wg': _L0_ffn_in['Wg'], 'L0_ffn_bg': _L0_ffn_in['bg'], 'L0_ffn_We': _L0_ffn_in['We'], 'L0_ffn_be': _L0_ffn_in['be'], 'L0_c': _L0_c, 'L0_wmod': _L0_wmod, 'L1_attn_W_qkv': _L1_attn_in['W_qkv'], 'L1_attn_b_qkv': _L1_attn_in['b_qkv'], 'L1_attn_W_out': _L1_attn_in['W_out'], 'L1_attn_b_out': _L1_attn_in['b_out'], 'L1_ffn_ln1_w': _L1_ffn_in['ln1_w'], 'L1_ffn_c_attn_w': _L1_ffn_in['c_attn_w'], 'L1_ffn_c_proj_w': _L1_ffn_in['c_proj_w'], 'L1_ffn_ln2_w': _L1_ffn_in['ln2_w'], 'L1_ffn_router_w': _L1_ffn_in['router_w'], 'L1_ffn_w1': _L1_ffn_in['w1'], 'L1_ffn_w2': _L1_ffn_in['w2'], 'L1_c': _L1_c, 'L1_wmod': _L1_wmod}
    _x0 = _d['L0_attn_x']
    _d['L0_attn_x'] = jax.random.normal(jax.random.fold_in(jax.random.key(seed), 1), (4, 1024, 256), dtype=_x0.dtype)
    del _x0
    return _d

def reference(L0_attn_x, L0_attn_Wq, L0_attn_bq, L0_attn_Wk, L0_attn_bk, L0_attn_Wv, L0_attn_bv, L0_attn_Wo, L0_attn_bo, L0_ffn_Wg, L0_ffn_bg, L0_ffn_We, L0_ffn_be, L0_c, L0_wmod, L1_attn_W_qkv, L1_attn_b_qkv, L1_attn_W_out, L1_attn_b_out, L1_ffn_ln1_w, L1_ffn_c_attn_w, L1_ffn_c_proj_w, L1_ffn_ln2_w, L1_ffn_router_w, L1_ffn_w1, L1_ffn_w2, L1_c, L1_wmod):

    def _L0_attn_ref(x, Wq, bq, Wk, bk, Wv, bv, Wo, bo):
        import math
        import jax, jax.numpy as jnp
        import numpy as np
        D_MODEL = 256
        NUM_HEADS = 16
        D_HEAD = D_MODEL // NUM_HEADS
        K_S = 32
        B, N = (2, 512)

        def _attn(x, Wq, bq, Wk, bk, Wv, bv, Wo, bo):
            b, n, _ = x.shape
            q = (x @ Wq.T + bq).reshape(b, n, NUM_HEADS, D_HEAD).transpose(0, 2, 1, 3)
            k = (x @ Wk.T + bk).reshape(b, n, NUM_HEADS, D_HEAD).transpose(0, 2, 1, 3)
            v = (x @ Wv.T + bv).reshape(b, n, NUM_HEADS, D_HEAD).transpose(0, 2, 1, 3)
            scores = jnp.einsum('bhqd,bhkd->bhqk', q, k) / math.sqrt(D_HEAD)
            causal = jnp.triu(jnp.ones((n, n), dtype=bool), k=1)
            neg_inf = jnp.array(-jnp.inf, dtype=scores.dtype)
            scores = jnp.where(causal, neg_inf, scores)
            vals, idx = jax.lax.top_k(scores, K_S)
            masked = jnp.full_like(scores, -jnp.inf)
            masked = jnp.put_along_axis(masked, idx, vals, axis=-1, inplace=False)
            attn = jax.nn.softmax(masked, axis=-1)
            out = jnp.einsum('bhqk,bhkd->bhqd', attn, v)
            out = out.transpose(0, 2, 1, 3).reshape(b, n, D_MODEL)
            y = out @ Wo.T + bo
            return (y, attn.mean(axis=1))

        def _reference_tuple_inner(x, Wq, bq, Wk, bk, Wv, bv, Wo, bo):
            return _attn(x, Wq, bq, Wk, bk, Wv, bv, Wo, bo)
        return _reference_tuple_inner(x, Wq, bq, Wk, bk, Wv, bv, Wo, bo)[0]

    def _L0_ffn_ref(x, Wg, bg, We, be):
        import jax, jax.numpy as jnp
        import numpy as np
        B, S, D, E = (4, 1024, 256, 8)
        probs = jax.nn.softmax(x @ Wg + bg, axis=-1)
        idx = jnp.argmax(probs, axis=-1)
        p = jnp.take_along_axis(probs, idx[..., None], axis=-1)[..., 0]
        e_idx = idx % We.shape[0]
        h = jax.nn.relu(jnp.einsum('bsd,edf->besf', x, We) + be[None, :, None, :])
        onehot = jax.nn.one_hot(e_idx, We.shape[0], dtype=x.dtype)
        out = jnp.einsum('besf,bse->bsf', h, onehot) * p[..., None]
        return out

    def _L1_attn_ref(x, W_qkv, b_qkv, W_out, b_out):
        import jax, jax.numpy as jnp
        import numpy as np
        HIDDEN = 256
        NUM_HEADS = 16
        HEAD_SIZE = 64
        B, S, _ = x.shape
        qkv = x @ W_qkv + b_qkv
        qkv = qkv.reshape(B, S, 3 * NUM_HEADS, HEAD_SIZE)
        Q = qkv[:, :, :NUM_HEADS, :]
        K = qkv[:, :, NUM_HEADS:2 * NUM_HEADS, :]
        V = qkv[:, :, 2 * NUM_HEADS:, :]
        scores = jnp.einsum('bqhi,bkhi->bhqk', Q, K) / jnp.sqrt(jnp.float32(HEAD_SIZE))
        mask = jnp.triu(jnp.full((S, S), -10000.0, dtype=scores.dtype), k=1)
        scores = scores + mask
        probs = jax.nn.softmax(scores, axis=-1)
        vals = jnp.einsum('bkhi,bhqk->bqhi', V, probs)
        vals = vals.reshape(B, S, NUM_HEADS * HEAD_SIZE)
        return vals @ W_out + b_out

    def _L1_ffn_ref(x, ln1_w, c_attn_w, c_proj_w, ln2_w, router_w, w1, w2):
        import jax, jax.numpy as jnp
        import numpy as np
        B, T, C, H, E, K, F = (2, 512, 256, 16, 8, 2, 512)
        EPS = 1e-05

        def layernorm(x, w):
            m = x.mean(-1, keepdims=True)
            v = x.var(-1, keepdims=True)
            return (x - m) * jax.lax.rsqrt(v + EPS) * w

        def attention(x, c_attn_w, c_proj_w):
            b, t, c = x.shape
            hd = c // H
            q, k, v = jnp.split(x @ c_attn_w, 3, axis=-1)
            q = q.reshape(b, t, H, hd).transpose(0, 2, 1, 3)
            k = k.reshape(b, t, H, hd).transpose(0, 2, 1, 3)
            v = v.reshape(b, t, H, hd).transpose(0, 2, 1, 3)
            att = jnp.einsum('bhqd,bhkd->bhqk', q, k) / jnp.sqrt(jnp.asarray(hd, x.dtype))
            causal = jnp.tril(jnp.ones((t, t), bool))
            att = jnp.where(causal, att, jnp.asarray(-jnp.inf, att.dtype))
            att = jax.nn.softmax(att, axis=-1)
            y = jnp.einsum('bhqk,bhkd->bhqd', att, v)
            y = y.transpose(0, 2, 1, 3).reshape(b, t, c)
            return y @ c_proj_w

        def moe_mlp(x, router_w, w1, w2):
            b, t, c = x.shape
            xf = x.reshape(-1, c)
            router_logits = xf @ router_w
            probs = jax.nn.softmax(router_logits.astype(jnp.float32), axis=-1)
            rw, sel = jax.lax.top_k(probs, K)
            rw = rw / rw.sum(axis=-1, keepdims=True)
            rw = rw.astype(x.dtype)
            w1e = w1.reshape(c, E, F).transpose(1, 0, 2)
            w2e = w2.reshape(E, F, c)
            h = jax.nn.gelu(jnp.einsum('nc,ecf->enf', xf, w1e), approximate=False)
            y_all = jnp.einsum('enf,efc->nec', h, w2e)
            y_sel = jnp.take_along_axis(y_all, sel[:, :, None], axis=1)
            y = (y_sel * rw[:, :, None]).sum(axis=1)
            return y.reshape(b, t, c)
        x = x + attention(layernorm(x, ln1_w), c_attn_w, c_proj_w)
        x = x + moe_mlp(layernorm(x, ln2_w), router_w, w1, w2)
        return x
    x = L0_attn_x
    mod = (_silu(L0_c) @ L0_wmod).reshape(L0_c.shape[0], 6, 1, -1)
    sa, ca, ga, sb, cb, gb = (mod[:, 0], mod[:, 1], mod[:, 2], mod[:, 3], mod[:, 4], mod[:, 5])
    ga = (2 * (ga >= 0) - 1) * jnp.maximum(jnp.abs(ga), 0.25)
    gb = (2 * (gb >= 0) - 1) * jnp.maximum(jnp.abs(gb), 0.25)
    h = _layernorm(x, axis=-1) * (1 + ca) + sa
    x = x + ga * _L0_attn_ref(h, L0_attn_Wq, L0_attn_bq, L0_attn_Wk, L0_attn_bk, L0_attn_Wv, L0_attn_bv, L0_attn_Wo, L0_attn_bo)
    h = _layernorm(x, axis=-1) * (1 + cb) + sb
    x = x + gb * _L0_ffn_ref(h, L0_ffn_Wg, L0_ffn_bg, L0_ffn_We, L0_ffn_be)
    mod = (_silu(L1_c) @ L1_wmod).reshape(L1_c.shape[0], 6, 1, -1)
    sa, ca, ga, sb, cb, gb = (mod[:, 0], mod[:, 1], mod[:, 2], mod[:, 3], mod[:, 4], mod[:, 5])
    ga = (2 * (ga >= 0) - 1) * jnp.maximum(jnp.abs(ga), 0.25)
    gb = (2 * (gb >= 0) - 1) * jnp.maximum(jnp.abs(gb), 0.25)
    h = _layernorm(x, axis=-1) * (1 + ca) + sa
    x = x + ga * _L1_attn_ref(h, L1_attn_W_qkv, L1_attn_b_qkv, L1_attn_W_out, L1_attn_b_out)
    h = _layernorm(x, axis=-1) * (1 + cb) + sb
    x = x + gb * _L1_ffn_ref(h, L1_ffn_ln1_w, L1_ffn_c_attn_w, L1_ffn_c_proj_w, L1_ffn_ln2_w, L1_ffn_router_w, L1_ffn_w1, L1_ffn_w2)
    return x

_drawn_inputs = setup_inputs


def setup_inputs(seed=0):
    import zlib

    import numpy as np

    out = dict(_drawn_inputs(seed))
    spreads = {'L0_attn_bq': (0.0, 0.642),
     'L0_attn_bk': (0.0, 0.8),
     'L0_attn_bv': (0.0, 0.296),
     'L0_attn_bo': (0.0, 0.297),
     'L0_ffn_bg': (0.0, 0.8),
     'L0_ffn_be': (0.0, 0.8),
     'L1_attn_b_qkv': (0.0, 0.1),
     'L1_attn_b_out': (0.0, 0.325),
     'L1_ffn_ln1_w': (1.0, 0.6),
     'L1_ffn_ln2_w': (1.0, 0.6)}
    factors = {'L0_ffn_Wg': 8.0,
     'L0_ffn_We': 8.0,
     'L1_ffn_c_attn_w': 8.0,
     'L1_ffn_c_proj_w': 8.0,
     'L1_ffn_router_w': 4.763,
     'L1_ffn_w1': 4.223,
     'L1_ffn_w2': 4.106}
    for name, (base, spread) in spreads.items():
        noise = np.random.default_rng([zlib.crc32(name.encode()), seed]).standard_normal(out[name].shape)
        drawn = base * np.exp(spread * noise) if base else spread * noise
        out[name] = jnp.asarray(drawn.astype(out[name].dtype))
    for name, factor in factors.items():
        out[name] = (out[name] * factor).astype(out[name].dtype)
    return out
```

```python
from contextlib import ExitStack

import concourse.bass as bass
from concourse import mybir

F32 = mybir.dt.float32
BF16 = mybir.dt.bfloat16
U32 = mybir.dt.uint32
ALU = mybir.AluOpType
ACT = mybir.ActivationFunctionType
AX = mybir.AxisListType.X

P = 128
B = 4
N = 1024
D = 256
NT = N // P
KC = D // P
EPS = 1e-5
TOPK = 32
E = 8
F = 512
FC = F // P
NEG_REPLACED = -3.0e38


class Attn:

    def __init__(self, name, slot, head, topk, bias, mask):
        self.name, self.slot, self.topk, self.bias = name, slot, topk, bias
        self.hg = P // slot
        self.groups = 16 // self.hg
        self.scale = float(head) ** -0.5
        self.mask = mask
        self.q_at = 0 if slot == 32 else 4
        self.units = NT * self.hg
        self.pairs = self.units // 2
        self.chunks = [(i // 4 + 1) for i in range(NT) for _ in range(self.hg)]
        self.chunk_at = [sum(self.chunks[:u]) for u in range(self.units + 1)]

    def unit(self, u):
        return u // self.hg, u % self.hg


A0 = Attn("a0", 32, 16, True, True, 0)
A1 = Attn("a1", 64, 64, False, True, 1)
A2 = Attn("a2", 32, 16, False, False, 0)
LNS = ["n0", "n1", "n2", "n3", "n4", "n5"]


class Chain:

    def __init__(self, eng, sem):
        self.eng, self.sem, self.n = eng, sem, 0

    def mark(self, ins):
        ins.then_inc(self.sem, 1)
        self.n += 1
        return self.n

    def need(self, n):
        self.eng.wait_ge(self.sem, n)

    def restart(self):
        self.eng.wait_ge(self.sem, self.n)
        self.eng.sem_clear(self.sem)
        self.n = 0


def build(nc, x, ct, wmod, wqkv, bqk, bv, wo, bo, ffn_wg, ffn_bg, ffn_we, ffn_be, ln_w, router_w, w1, w2, out):
    ctx = ExitStack()
    with ctx:
        def sb(name, shape, dt=F32):
            return ctx.enter_context(nc.sbuf_tensor(name, shape, dt))

        def ps(name, shape, dt=F32):
            return ctx.enter_context(nc.psum_tensor(name, shape, dt))

        def sem(name):
            return ctx.enter_context(nc.semaphore(name))

        mod_dram = nc.dram_tensor("mod_rows", (B, 2, 6, D), F32, kind="Internal").ap()

        pA = [ps(f"pA{i}", [P, N]) for i in range(2)]
        pT = [ps(f"pT{i}", [P, 512]) for i in range(2)]
        pO = ps("pO", [P, N])

        ident = sb("ident", [P, P])
        identm = sb("identm", [P, P], BF16)
        tri = sb("tri", [P, 2, P], BF16)
        iota8 = sb("iota8", [P, E])
        mhalf = sb("mhalf", [P, NT])
        ctile = sb("ctile", [P, 2, KC, B])
        csig = sb("csig", [P, 2, KC, B])
        wg = sb("wg", [P, KC, D])
        bg_bc = sb("bg_bc", [P, D])
        we = sb("we", [P, KC, E, D])
        be = sb("be", [E, D])
        lnw = sb("lnw", [P, 2, KC])
        rw = sb("rw", [P, KC, E])
        bo_bc = sb("bo_bc", [P, 2, D])

        X = sb("X", [P, NT, D])
        Z = sb("Z", [P, NT, D])
        xn = sb("xn", [P, NT, D])
        hT = sb("hT", [P, KC, N])
        fmr = sb("fmr", [P, P])
        fm = sb("fm", [P, 2, 6, KC])
        bc = sb("bc", [P, 6, D])
        st = sb("st", [P, NT, 6])
        mv = sb("mv", [P, NT, 2])
        ve = sb("ve", [P, NT])
        rstd = sb("rstd", [P, NT])

        wq = sb("wq", [P, KC, 3 * P])
        bqk_sb = sb("bqk_sb", [P, 2])
        bq_s = sb("bq_s", [P, 1])
        bv_bc = sb("bv_bc", [P, P])
        wo_sb = sb("wo_sb", [P, 8, D])
        qm = sb("qm", [P, 6, N])
        kT = sb("kT", [P, N])
        vs = sb("vs", [P, NT, P])
        oall = sb("oall", [P, 8, N])
        ssb = sb("ssb", [P, 4, N])
        work = sb("work", [P, 2, N])
        pr = sb("pr", [P, 4, N])
        prT = sb("prT", [P, 4, N])
        vals = sb("vals", [P, 4, TOPK])
        nmax = sb("nmax", [P, 4])
        rsum = sb("rsum", [P, 32])
        rinv = sb("rinv", [P, 32])
        rbc = work[:, 0, :]

        lg = ssb[:, 0:2, :].rearrange("p a (t d) -> p (a t) d", d=D)
        v8 = sb("v8", [P, NT, 8])
        ix8 = sb("ix8", [P, NT, 8], U32)
        ixf = sb("ixf", [P, NT, 2])
        gsm = sb("gsm", [P, NT, 8])
        gate = sb("gate", [P, NT, E])
        gate2 = sb("gate2", [P, NT, E])
        gT = sb("gT", [E, N])
        acc = [work[:, 1, i * D:(i + 1) * D] for i in range(4)]
        tmp = [sb(f"tmp{i}", [P, D]) for i in range(2)]
        H = [pr[:, 2 * i:2 * i + 2, :].rearrange("p a (f n) -> p (a f) n", n=512) for i in range(2)]
        w1_sb = [ssb[:, i, :].rearrange("p (k f) -> p k f", k=KC) for i in range(2)]
        w2_sb = [ssb[:, 2 + i, :].rearrange("p (k f) -> p k f", k=FC) for i in range(2)]
        wm_sb = [oall[:, 3 * i:3 * i + 3, :].rearrange("p a n -> p (a n)").rearrange("p (k n) -> p k n", k=KC)
                 for i in range(2)]
        modrow = oall[0:B, 6:8, :].rearrange("p a n -> p (a n)")[:, 0:6 * D]
        modtmp = ssb[0:B, 0, 0:D]
        modsgn = ssb[0:B, 1, 0:D]

        s_const = sem("s_const")
        s_wld = sem("s_wld")
        s_mld = sem("s_mld")
        s_cexp = sem("s_cexp")
        s_csil = sem("s_csil")
        s_mmm = sem("s_mmm")
        s_mrow = sem("s_mrow")
        s_mst = sem("s_mst")
        s_bld = sem("s_bld")
        s_fmt = sem("s_fmt")
        s_fm = sem("s_fm")
        s_fin = sem("s_fin")
        s_out = sem("s_out")
        dv = sem("dv")
        ac = sem("ac")
        ln = {}
        for n in LNS:
            ln[n] = {k: sem(f"{n}_{k}") for k in (
                "var",
                "rs",
                "xn",
                "tr",
                "ev",
            )}
        at = {}
        for a in (A0, A1, A2):
            at[a.name] = {k: sem(f"{a.name}_{k}") for k in (
                "w",
                "wo",
                "pj",
                "bs",
                "eqk",
                "ev",
                "s",
                "cp",
                "mx",
                "e",
                "p",
                "t",
                "te",
                "pv",
                "ri",
                "bc",
                "be",
                "o",
                "y",
                "x",
            )}
        f0 = {k: sem(f"f0_{k}") for k in (
            "lg",
            "le",
            "nm",
            "se",
            "g",
            "gt",
            "ge",
            "y",
            "yb",
            "yc",
            "x",
        )}
        m1 = {k: sem(f"m1_{k}") for k in (
            "w0",
            "w1",
            "lg",
            "df",
            "e1",
            "g",
            "h",
            "ge",
            "y",
            "z",
        )}

        gw_d = {a.name: wqkv[n] for n, a in enumerate((A0, A1, A2))}
        block = ctx.enter_context(nc.Block())

        @block.sync
        def _(sp):
            sp.dma_start(ctile[:, :, :, :], ct).then_inc(s_mld, 16)
            for l in range(2):
                sp.dma_start(wm_sb[l], wmod[l].rearrange("(k p) n -> p k n", p=P)).then_inc(s_mld, 16)
            for dst, src in (
                (wg[:, :, :], ffn_wg.rearrange("(k p) n -> p k n", p=P)),
                (bg_bc[:, :], ffn_bg.partition_broadcast(P)),
                (we[:, :, :, :], ffn_we),
                (be[:, :], ffn_be),
                (lnw[:, :, :], ln_w),
                (rw[:, :, :], router_w.rearrange("(k p) n -> p k n", p=P)),
                (bo_bc[:, 0, :], bo[0].partition_broadcast(P)),
                (bo_bc[:, 1, :], bo[1].partition_broadcast(P)),
            ):
                sp.dma_start(dst, src).then_inc(s_wld, 16)
            for l in range(2):
                sp.wait_ge(s_mrow, l + 1)
                sp.dma_start(mod_dram[:, l],
                             modrow.rearrange("b (j d) -> b j d", j=6)).then_inc(s_mst, 16)
            sp.wait_ge(s_mst, 32)

            def group_weights(a, g):
                s = at[a.name]
                sp.dma_start(wq[:, :, :], gw_d[a.name][bass.ds(g, 1)].rearrange("a p k n -> (a p) k n"))\
                  .then_inc(s["w"], 16)
                if a.bias:
                    i = 0 if a is A0 else 1
                    sp.dma_start(bqk_sb[:, :], bqk[i][bass.ds(g, 1)].rearrange("a p n -> (a p) n"))\
                      .then_inc(s["w"], 16)
                    sp.dma_start(bv_bc[:, :], bv[i][bass.ds(g, 1)].partition_broadcast(P)
                                 .rearrange("p a n -> p (a n)")).then_inc(s["w"], 16)

            with sp.Fori(0, B) as b:
                sp.wait_ge(s_out, b * 16)
                sp.dma_start(X[:, :, :], x[bass.ds(b, 1)].rearrange("a (t p) d -> p (a t) d", p=P))\
                  .then_inc(s_bld, 16)
                sp.dma_start(fmr[0:24, :], mod_dram[bass.ds(b, 1)]
                             .rearrange("a l j (c p) -> (a l j c) p", p=P)).then_inc(s_bld, 16)
                for i, (l, j) in enumerate(((0, 2), (0, 5), (1, 2), (1, 3), (1, 4), (1, 5))):
                    sp.dma_start(bc[:, i, :], mod_dram[bass.ds(b, 1), l, j, :].partition_broadcast(P)
                                 .rearrange("p a n -> p (a n)")).then_inc(s_bld, 16)
                prev = None
                for n, a in enumerate((A0, A1, A2)):
                    if prev is not None:
                        sp.wait_ge(at[prev.name]["y"], b * NT + NT)
                    sp.dma_start(wo_sb[:, 0:a.groups, :], wo[n]).then_inc(at[a.name]["wo"], 16)
                    group_weights(a, 0)
                    with sp.Fori(0, a.groups - 1) as g:
                        sp.wait_ge(at[a.name]["s"], (b * a.groups + g) * a.units + 1)
                        group_weights(a, g + 1)
                    prev = a
                sp.wait_ge(m1["df"], b + 1)

                def expert(par, e):
                    sp.dma_start(w1_sb[par], w1[bass.ds(e, 1)].rearrange("a p k n -> (a p) k n"))\
                      .then_inc(m1["w%d" % par], 16)
                    sp.dma_start(w2_sb[par], w2[bass.ds(e, 1)].rearrange("a p k n -> (a p) k n"))\
                      .then_inc(m1["w%d" % par], 16)

                expert(0, 0)
                with sp.Fori(0, E // 2 - 1) as ep:
                    it = b * (E // 2) + ep
                    sp.wait_ge(m1["y"], it * 2 * NT)
                    expert(1, ep * 2 + 1)
                    sp.wait_ge(m1["y"], it * 2 * NT + NT)
                    expert(0, ep * 2 + 2)
                sp.wait_ge(m1["y"], (b * (E // 2) + E // 2 - 1) * 2 * NT)
                expert(1, E - 1)
                sp.wait_ge(s_fin, b + 1)
                sp.dma_start(out[bass.ds(b, 1)].rearrange("a (t p) d -> p (a t) d", p=P), X[:, :, :])\
                  .then_inc(s_out, 16)
            sp.wait_ge(s_out, B * 16)

        @block.gpsimd
        def _(pool):
            c = Chain(pool, s_const)
            c.mark(pool.memset(ident[:, :], 0.0))
            c.mark(pool.memset(identm[:, :], 0.0))
            c.mark(pool.memset(tri[:, :, :], 0.0))
            c.mark(pool.memset(mhalf[:, :], -0.5))
            c.mark(pool.memset(qm[:, :, :], 0.0))
            c.mark(pool.memset(fmr[:, :], 0.0))
            c.mark(pool.iota(iota8[:, :], pattern=[[1, E]], base=0, channel_multiplier=0,
                             allow_small_or_imprecise_dtypes=True))
            c.need(c.n)
            c.mark(pool.affine_select(out=ident[:, :], in_=ident[:, :], compare_op=ALU.not_equal, fill=1.0,
                                      base=0, pattern=[[-1, P]], channel_multiplier=1))
            c.mark(pool.affine_select(out=identm[:, :], in_=identm[:, :], compare_op=ALU.not_equal, fill=80.0,
                                      base=0, pattern=[[-1, P]], channel_multiplier=1))
            for m, value in ((0, -(2.0 ** 90)), (1, -125.0)):
                c.mark(pool.affine_select(out=tri[:, m, :], in_=tri[:, m, :], compare_op=ALU.is_ge, fill=value,
                                          base=0, pattern=[[-1, P]], channel_multiplier=1))
            with pool.Fori(0, B) as b:
                for n in LNS:
                    pool.wait_ge(ln[n]["var"], b + 1)
                    pool.tensor_tensor(rstd[:, :], ve[:, :], mhalf[:, :], ALU.pow).then_inc(ln[n]["rs"], 1)
        N_CONST = 11

        @block.scalar
        def _(act):
            chain = Chain(act, ac)
            act.wait_ge(s_mld, 48)
            act.activation(csig[:, :, :, :], ctile[:, :, :, :], ACT.Exp, scale=-1.0).then_inc(s_cexp, 1)
            act.wait_ge(s_wld, 16 * 8)

            def norm(n, b, scale, shift):
                s = ln[n]
                for idx in range(4):
                    half, c = idx // 2, idx % 2
                    act.wait_ge(s["tr"], b * 4 + idx + 1)
                    act.activation(hT[:, c, half * 512:half * 512 + 512], pT[idx % 2][:, :], ACT.Identity,
                                   scale=scale[:, c:c + 1],
                                   bias=shift[:, c:c + 1] if shift is not None else 0.0).then_inc(s["ev"], 1)

            def attention(a, b):
                s = at[a.name]
                U, CH = a.units, a.chunk_at[-1]
                nw = 48 if a.bias else 16
                with act.Fori(0, a.groups) as g:
                    it = b * a.groups + g
                    act.wait_ge(s["w"], it * nw + nw)
                    if a.bias:
                        act.mul(bq_s[:, :], bqk_sb[:, 0:1], a.scale).then_inc(s["bs"], 1)
                        act.wait_ge(s["bs"], it + 1)
                    act.wait_ge(s["pj"], it * 3 + 1)
                    for j in range(a.hg):
                        sl = slice(j * a.slot, (j + 1) * a.slot)
                        act.activation(qm[sl, a.q_at + j, :], pA[0][sl, :], ACT.Identity, scale=a.scale,
                                       bias=bq_s[sl, :] if a.bias else 0.0).then_inc(s["eqk"], 1)
                    act.wait_ge(s["pj"], it * 3 + 2)
                    act.activation(kT[:, :], pA[1][:, :], ACT.Identity,
                                   bias=bqk_sb[:, 1:2] if a.bias else 0.0).then_inc(s["eqk"], 1)

                    def copy(u):
                        i, j = a.unit(u)
                        w = (i + 1) * P
                        act.wait_ge(s["s"], it * U + u + 1)
                        act.wait_ge(s["p"], it * U + max(u - 3, 0))
                        act.activation(ssb[:, u % 4, 0:w], pA[u % 2][:, 0:w], ACT.Copy).then_inc(s["cp"], 1)

                    def exp_topk(u):
                        i, j = a.unit(u)
                        w = (i + 1) * P
                        act.wait_ge(s["mx"], it * a.pairs + u // 2 + 1)
                        act.wait_ge(s["t"], it * CH + a.chunk_at[max(u - 3, 0)])
                        act.activation(pr[:, u % 4, 0:w], ssb[:, u % 4, 0:w], ACT.Exp,
                                       bias=nmax[:, u % 4:u % 4 + 1]).then_inc(s["e"], 1)

                    def exp_plain(u):
                        i, j = a.unit(u)
                        w = (i + 1) * P
                        act.wait_ge(s["s"], it * U + u + 1)
                        act.wait_ge(s["mx"], it * U + u + 1)
                        act.wait_ge(s["t"], it * CH + a.chunk_at[max(u - 3, 0)])
                        act.activation(pr[:, u % 4, 0:w], pA[u % 2][:, 0:w], ACT.Exp,
                                       bias=nmax[:, u % 4:u % 4 + 1],
                                       accum_out=rsum[:, u:u + 1]).then_inc(s["e"], 1)

                    def out_of_psum(u):
                        i, j = a.unit(u)
                        for c in range(a.chunks[u]):
                            q = a.chunk_at[u] + c
                            w = min(i + 1 - 4 * c, 4) * P
                            act.wait_ge(s["t"], it * CH + q + 1)
                            act.wait_ge(s["pv"], it * a.pairs + max(u // 2 - 1, 0))
                            act.activation(prT[:, u % 4, c * 512:c * 512 + w], pT[q % 2][:, 0:w], ACT.Copy)\
                               .then_inc(s["te"], 1)

                    if a.topk:
                        for u in range(4):
                            copy(u)
                        for p in range(a.pairs):
                            for u in (2 * p, 2 * p + 1):
                                exp_topk(u)
                            if p >= 1:
                                for u in (2 * p - 2, 2 * p - 1):
                                    out_of_psum(u)
                                    if u + 4 < U:
                                        copy(u + 4)
                        for u in (U - 2, U - 1):
                            out_of_psum(u)
                    else:
                        for u in range(U):
                            exp_plain(u)
                    act.wait_ge(s["bc"], it + 1)
                    act.wait_ge(s["o"], it)
                    act.activation(rbc, pA[0][:, :], ACT.Copy).then_inc(s["be"], 1)

            with act.Fori(0, B) as b:
                act.wait_ge(s_fmt, b + 1)
                act.activation(fm[:, :, :, :].rearrange("p l j c -> p (l j c)"), pT[0][:, 0:24], ACT.Copy)\
                   .then_inc(s_fm, 1)
                act.wait_ge(s_fm, b + 1)
                norm("n0", b, fm[:, 0, 1, :], fm[:, 0, 0, :])
                attention(A0, b)
                norm("n1", b, fm[:, 0, 4, :], fm[:, 0, 3, :])
                act.wait_ge(f0["nm"], b + 1)
                for t in range(NT):
                    act.activation(lg[:, t, :], lg[:, t, :], ACT.Exp, bias=gsm[:, t, 0:1],
                                   accum_out=gsm[:, t, 1:2]).then_inc(f0["se"], 1)
                norm("n2", b, fm[:, 1, 1, :], fm[:, 1, 0, :])
                attention(A1, b)
                norm("n4", b, lnw[:, 0, :], None)
                attention(A2, b)
                norm("n5", b, lnw[:, 1, :], None)
                act.wait_ge(m1["df"], b + 1)
                act.activation(gsm[:, :, 1], gsm[:, :, 0], ACT.Exp).then_inc(m1["e1"], 1)
                with act.Fori(0, E // 2) as ep:
                    it = b * (E // 2) + ep
                    for par in range(2):
                        for half in range(2):
                            for f in range(FC):
                                q = (par * 2 + half) * FC + f
                                act.wait_ge(m1["h"], it * 4 * FC + q + 1)
                                act.wait_ge(m1["y"], it * 2 * NT + max((par * 2 + half - 1) * 4, 0))
                                act.activation(H[half][:, f, :], pA[q // 2 % 2][:, q % 2 * 512:q % 2 * 512 + 512],
                                               ACT.Gelu).then_inc(m1["ge"], 1)

        @block.tensor
        def _(pe):
            pe.wait_ge(s_const, N_CONST)
            pe.wait_ge(s_csil, 1)
            for l in range(2):
                if l:
                    pe.wait_ge(s_mrow, 1)
                for c in range(3):
                    for k in range(KC):
                        mm = pe.matmul(pA[c // 2][0:B, c % 2 * 512:c % 2 * 512 + 512], csig[:, l, k, :],
                                       wm_sb[l][:, k, c * 512:c * 512 + 512], start=(k == 0), stop=(k == KC - 1))
                mm.then_inc(s_mmm, 1)
            pe.wait_ge(s_wld, 16 * 8)

            def norm(n, b):
                s = ln[n]
                for idx in range(4):
                    half, c = idx // 2, idx % 2
                    if c == 0:
                        pe.wait_ge(s["xn"], b * NT + 4 * half + 4)
                    if idx >= 2:
                        pe.wait_ge(s["ev"], b * 4 + idx - 1)
                    for t in range(4):
                        mm = pe.transpose(pT[idx % 2][:, t * P:t * P + P],
                                          xn[:, 4 * half + t, c * P:c * P + P], ident[:, :])
                    mm.then_inc(s["tr"], 1)

            def attention(a, b, n):
                s = at[a.name]
                U, CH = a.units, a.chunk_at[-1]
                nw = 48 if a.bias else 16
                done = s["cp"] if a.topk else s["e"]
                with pe.Fori(0, a.groups) as g:
                    pe.wait_ge(ln[n]["ev"], b * 4 + 4)
                    it = b * a.groups + g
                    pe.wait_ge(s["w"], it * nw + nw)
                    pe.wait_ge(s["be"], it)
                    pe.wait_ge(done, it * U)
                    for w in range(2):
                        for h in range(2):
                            for k in range(KC):
                                mm = pe.matmul(pA[w][:, h * 512:h * 512 + 512], wq[:, k, w * P:w * P + P],
                                               hT[:, k, h * 512:h * 512 + 512],
                                               start=(k == 0), stop=(k == KC - 1))
                        mm.then_inc(s["pj"], 1)
                    pe.wait_ge(s["eqk"], it * (a.hg + 1) + a.hg)
                    for t in range(NT):
                        for k in range(KC):
                            mm = pe.matmul(pA[0][:, t * P:t * P + P], hT[:, k, t * P:t * P + P],
                                           wq[:, k, 2 * P:3 * P], start=(k == 0), stop=(k == KC - 1))
                    mm.then_inc(s["pj"], 1)
                    pe.wait_ge(s["eqk"], it * (a.hg + 1) + a.hg + 1)
                    pe.wait_ge(s["ev"], it + 1)

                    def scores(u):
                        i, j = a.unit(u)
                        if u >= 2:
                            pe.wait_ge(done, it * U + u - 1)
                        w = (i + 1) * P
                        for lo in range(0, w, 512):
                            hi = min(lo + 512, w)
                            mm = pe.matmul(pA[u % 2][:, lo:hi], qm[:, a.q_at + j, i * P:i * P + P], kT[:, lo:hi],
                                           start=True, stop=(hi < w))
                        mm = pe.matmul(pA[u % 2][:, w - P:w], identm[:, :], tri[:, a.mask, :],
                                       start=False, stop=True)
                        mm.then_inc(s["s"], 1)

                    def turn(u):
                        i, j = a.unit(u)
                        pe.wait_ge(s["p"] if a.topk else s["e"], it * U + u + 1)
                        for c in range(a.chunks[u]):
                            q = a.chunk_at[u] + c
                            pe.wait_ge(s["te"], it * CH + max(q - 1, 0))
                            for kb in range(4 * c, min(4 * c + 4, i + 1)):
                                mm = pe.transpose(pT[q % 2][:, kb % 4 * P:kb % 4 * P + P],
                                                  pr[:, u % 4, kb * P:kb * P + P], ident[:, :])
                            mm.then_inc(s["t"], 1)

                    def values(p):
                        i, j = a.unit(2 * p)
                        pe.wait_ge(s["te"], it * CH + a.chunk_at[2 * p + 2])
                        if p == 0:
                            pe.wait_ge(s["o"], it)
                        for kb in range(i + 1):
                            for u in (2 * p, 2 * p + 1):
                                j = a.unit(u)[1]
                                sl = slice(j * a.slot, (j + 1) * a.slot)
                                mm = pe.matmul(pO[sl, i * P:i * P + P], vs[:, kb, sl],
                                               prT[:, u % 4, kb * P:kb * P + P],
                                               start=(kb == 0), stop=(kb == i))
                        mm.then_inc(s["pv"], 1)

                    for u in range(2):
                        scores(u)
                    for p in range(a.pairs):
                        for u in (2 * p, 2 * p + 1):
                            if a.topk:
                                if u + 2 < U:
                                    scores(u + 2)
                            else:
                                turn(u)
                                if u + 2 < U:
                                    scores(u + 2)
                        if a.topk:
                            if p >= 1:
                                turn(2 * p - 2)
                                turn(2 * p - 1)
                            if p >= 2:
                                values(p - 2)
                        elif p >= 1:
                            values(p - 1)
                    if a.topk:
                        turn(U - 2)
                        turn(U - 1)
                        values(a.pairs - 2)
                    values(a.pairs - 1)
                    pe.wait_ge(s["ri"], it + 1)
                    pe.wait_ge(done, it * U + U)
                    for i in range(NT):
                        for j in range(a.hg):
                            sl = slice(j * a.slot, (j + 1) * a.slot)
                            u = i * a.hg + j
                            mm = pe.matmul(pA[0][sl, i * P:i * P + P],
                                           rinv[:, u:u + 1].to_broadcast([P, a.slot]), ident[:, :],
                                           start=True, stop=True)
                    mm.then_inc(s["bc"], 1)
                pe.wait_ge(s["o"], b * a.groups + a.groups)
                pe.wait_ge(s["wo"], b * 16 + 16)
                pe.wait_ge(s["te"], (b * a.groups + a.groups) * CH)
                for t in range(NT):
                    if t >= 2:
                        pe.wait_ge(s["x"], b * NT + t - 1)
                    for g in range(a.groups):
                        mm = pe.matmul(pT[t % 2][:, 0:D], oall[:, g, t * P:t * P + P], wo_sb[:, g, :],
                                       start=(g == 0), stop=(g == a.groups - 1))
                    mm.then_inc(s["y"], 1)

            with pe.Fori(0, B) as b:
                pe.wait_ge(s_bld, b * 128 + 128)
                pe.transpose(pT[0][:, 0:P], fmr[:, :], ident[:, :]).then_inc(s_fmt, 1)
                pe.wait_ge(s_fm, b + 1)
                norm("n0", b)
                attention(A0, b, "n0")
                norm("n1", b)
                pe.wait_ge(ln["n1"]["ev"], b * 4 + 4)
                for t in range(NT):
                    if t >= 2:
                        pe.wait_ge(f0["le"], b * NT + t - 1)
                    for k in range(KC):
                        mm = pe.matmul(pT[t % 2][:, 0:D], hT[:, k, t * P:t * P + P], wg[:, k, :],
                                       start=(k == 0), stop=(k == KC - 1))
                    mm.then_inc(f0["lg"], 1)
                pe.wait_ge(f0["g"], b + 1)
                for t in range(NT):
                    mm = pe.transpose(pT[t // 4][0:E, t % 4 * P:t % 4 * P + P], gate[:, t, :], ident[:, :])
                mm.then_inc(f0["gt"], 1)
                pe.wait_ge(f0["ge"], b * 2 + 2)
                for t in range(NT):
                    if t >= 2:
                        pe.wait_ge(f0["x"], b * NT + t - 1)
                    pe.matmul(pT[t % 2][:, 0:D], gT[:, t * P:t * P + P], be[:, :], start=True, stop=True)\
                      .then_inc(f0["yb"], 1)
                    for half in range(2):
                        if t >= 1:
                            pe.wait_ge(f0["yc"], b * 2 * NT + 2 * t + half - 1)
                        for e2 in range(2):
                            e = 4 * half + 2 * e2
                            for k in range(KC):
                                mm = pe.matmul(pA[half][:, e2 * 512:e2 * 512 + 512], hT[:, k, t * P:t * P + P],
                                               we[:, k, e:e + 2, :], start=(k == 0), stop=(k == KC - 1))
                        mm.then_inc(f0["y"], 1)
                norm("n2", b)
                attention(A1, b, "n2")
                norm("n4", b)
                attention(A2, b, "n4")
                norm("n5", b)
                pe.wait_ge(ln["n5"]["ev"], b * 4 + 4)
                for t in range(NT):
                    for k in range(KC):
                        mm = pe.matmul(pT[0][:, t * E:t * E + E], hT[:, k, t * P:t * P + P], rw[:, k, :],
                                       start=(k == 0), stop=(k == KC - 1))
                mm.then_inc(m1["lg"], 1)
                with pe.Fori(0, E // 2) as ep:
                    pe.wait_ge(m1["g"], b + 1)
                    it = b * (E // 2) + ep

                    def hidden(r):
                        par, half = r // 2, r % 2
                        if half == 0:
                            pe.wait_ge(m1["w%d" % par], it * 32 + 32)
                        for f in range(FC):
                            q = r * FC + f
                            pe.wait_ge(m1["ge"], it * 4 * FC + max(q - 3, 0))
                            for k in range(KC):
                                mm = pe.matmul(pA[q // 2 % 2][:, q % 2 * 512:q % 2 * 512 + 512],
                                               w1_sb[par][:, k, f * P:f * P + P],
                                               hT[:, k, half * 512:half * 512 + 512],
                                               start=(k == 0), stop=(k == KC - 1))
                            mm.then_inc(m1["h"], 1)

                    def down(r):
                        par, half = r // 2, r % 2
                        pe.wait_ge(m1["ge"], it * 4 * FC + (r + 1) * FC)
                        for t in range(4):
                            q = r * 4 + t
                            pe.wait_ge(m1["z"], it * 2 * NT + max(q - 1, 0))
                            for f in range(FC):
                                mm = pe.matmul(pT[q % 2][:, 0:D], H[half][:, f, t * P:t * P + P],
                                               w2_sb[par][:, f, :], start=(f == 0), stop=(f == FC - 1))
                            mm.then_inc(m1["y"], 1)

                    hidden(0)
                    for r in range(1, 4):
                        hidden(r)
                        down(r - 1)
                    down(3)

        @block.vector
        def _(v):
            ch = Chain(v, dv)
            v.wait_ge(s_cexp, 1)
            n = ch.mark(v.tensor_scalar(csig[:, :, :, :], csig[:, :, :, :], 1.0, None, ALU.add))
            ch.need(n)
            n = ch.mark(v.reciprocal(csig[:, :, :, :], csig[:, :, :, :]))
            ch.need(n)
            v.tensor_tensor(csig[:, :, :, :], csig[:, :, :, :], ctile[:, :, :, :], ALU.mult).then_inc(s_csil, 1)
            for l in range(2):
                v.wait_ge(s_mmm, l + 1)
                if l:
                    v.wait_ge(s_mst, 16)
                ch.mark(v.tensor_copy(modrow[:, 0:N], pA[0][0:B, :]))
                n = ch.mark(v.tensor_copy(modrow[:, N:6 * D], pA[1][0:B, 0:512]))
                ch.need(n)
                for j in (1, 4):
                    ch.mark(v.tensor_scalar(modrow[:, j * D:j * D + D], modrow[:, j * D:j * D + D], 1.0, None,
                                            ALU.add))
                for j in (2, 5):
                    r = modrow[:, j * D:j * D + D]
                    ch.mark(v.scalar_tensor_tensor(out=modtmp, in0=r, scalar=-1.0, in1=r, op0=ALU.mult,
                                                   op1=ALU.max))
                    n = ch.mark(v.tensor_scalar(modsgn, r, 0.0, 2.0, ALU.is_ge, ALU.mult))
                    ch.need(n)
                    n = ch.mark(v.tensor_scalar(modtmp, modtmp, 0.25, None, ALU.max))
                    ch.need(n)
                    n = ch.mark(v.scalar_tensor_tensor(out=r, in0=modsgn, scalar=-1.0, in1=modtmp, op0=ALU.add,
                                                       op1=ALU.mult))
                    ch.need(n)
                v.sem_inc(s_mrow, 1)
            ch.restart()
            v.wait_ge(s_wld, 16 * 8)
            v.wait_ge(s_const, N_CONST)

            def norm(n, b, src):
                s = ln[n]
                at0 = ch.n
                for t in range(NT):
                    ch.mark(v.bn_stats(st[:, t, :], src[:, t, :]))
                for t in range(NT):
                    ch.need(at0 + t + 1)
                    k = ch.mark(v.bn_aggr(mv[:, t, :], st[:, t, :]))
                ch.need(k)
                v.tensor_scalar(ve[:, :], mv[:, :, 1], EPS, None, ALU.add).then_inc(s["var"], 1)
                for t in range(NT):
                    if t == 0:
                        v.wait_ge(s["rs"], b + 1)
                    v.tensor_scalar(xn[:, t, :], src[:, t, :], mv[:, t, 0:1], rstd[:, t:t + 1],
                                    ALU.subtract, ALU.mult).then_inc(s["xn"], 1)

            def attention(a, b):
                s = at[a.name]
                U, CH = a.units, a.chunk_at[-1]
                nw = 48 if a.bias else 16
                ch.restart()
                with v.Fori(0, a.groups) as g:
                    it = b * a.groups + g
                    v.wait_ge(s["w"], it * nw + nw)
                    v.wait_ge(s["pj"], it * 3 + 3)
                    psv = pA[0][:, :].rearrange("p (t n) -> p t n", n=P)
                    if a.bias:
                        v.tensor_tensor(vs[:, :, :], psv, bv_bc[:, :].unsqueeze(1).to_broadcast([P, NT, P]),
                                        ALU.add).then_inc(s["ev"], 1)
                    else:
                        v.tensor_copy(vs[:, :, :], psv).then_inc(s["ev"], 1)

                    def select(p):
                        us = (2 * p, 2 * p + 1)
                        i = a.unit(us[0])[0]
                        w = (i + 1) * P
                        last = {}
                        for u in us:
                            last[u] = ch.mark(v.max(vals[:, u % 4, 0:8], ssb[:, u % 4, 0:w]))
                        ch.need(last[us[1]])
                        v.wait_ge(s["e"], it * U + max(us[0] - 2, 0))
                        c = us[0] % 4
                        v.tensor_scalar(nmax[:, c:c + 2], vals[:, c:c + 2, 0], -1.0, None, ALU.mult)\
                         .then_inc(s["mx"], 1)
                        for r in range(TOPK // 8 - 1):
                            for u in us:
                                ch.need(last[u])
                                src = ssb[:, u % 4, 0:w] if r == 0 else work[:, u % 2, 0:w]
                                last[u] = ch.mark(v.match_replace(
                                    out=work[:, u % 2, 0:w], in_to_replace=vals[:, u % 4, 8 * r:8 * r + 8],
                                    in_values=src, imm_value=NEG_REPLACED))
                            for u in us:
                                ch.need(last[u])
                                last[u] = ch.mark(v.max(vals[:, u % 4, 8 * r + 8:8 * r + 16],
                                                        work[:, u % 2, 0:w]))
                        for u in us:
                            ch.need(last[u])
                            v.wait_ge(s["e"], it * U + u + 1)
                            if u % 2 and u + 2 < U:
                                v.wait_ge(s["cp"], it * U + u + 3)
                            v.scalar_tensor_tensor(out=pr[:, u % 4, 0:w], in0=ssb[:, u % 4, 0:w],
                                                   scalar=vals[:, u % 4, TOPK - 1:TOPK],
                                                   in1=pr[:, u % 4, 0:w], op0=ALU.is_ge, op1=ALU.mult,
                                                   accum_out=rsum[:, u:u + 1]).then_inc(s["p"], 1)

                    def rowmax(u):
                        w = (a.unit(u)[0] + 1) * P
                        v.wait_ge(s["s"], it * U + u + 1)
                        v.wait_ge(s["e"], it * U + max(u - 3, 0))
                        v.tensor_reduce(nmax[:, u % 4:u % 4 + 1], pA[u % 2][:, 0:w], AX, ALU.max,
                                        negate=True).then_inc(s["mx"], 1)

                    def out_of_psum(u):
                        i, j = a.unit(u)
                        for c in range(a.chunks[u]):
                            q = a.chunk_at[u] + c
                            w = min(i + 1 - 4 * c, 4) * P
                            v.wait_ge(s["t"], it * CH + q + 1)
                            v.wait_ge(s["pv"], it * a.pairs + max(u // 2 - 1, 0))
                            v.tensor_copy(prT[:, u % 4, c * 512:c * 512 + w], pT[q % 2][:, 0:w])\
                             .then_inc(s["te"], 1)

                    if a.topk:
                        v.wait_ge(s["cp"], it * U + 2)
                        v.memset(rsum[:, :], 0.0)
                        for p in range(a.pairs):
                            select(p)
                        v.wait_ge(s["p"], it * U + U)
                    else:
                        rowmax(0)
                        for u in range(U):
                            if u + 1 < U:
                                rowmax(u + 1)
                            out_of_psum(u)
                        v.wait_ge(s["e"], it * U + U)
                    v.reciprocal(rinv[:, 0:U], rsum[:, 0:U]).then_inc(s["ri"], 1)
                    v.wait_ge(s["pv"], it * a.pairs + a.pairs)
                    v.wait_ge(s["be"], it + 1)
                    v.tensor_tensor(oall[:, bass.ds(g, 1), :].rearrange("p a n -> p (a n)"), pO[:, :], rbc,
                                    ALU.mult).then_inc(s["o"], 1)
                    ch.restart()

            def project(a, b, dst, bias, gate_row):
                s = at[a.name]
                for t in range(NT):
                    v.wait_ge(s["y"], b * NT + t + 1)
                    y = pT[t % 2][:, 0:D]
                    if bias is not None:
                        n = ch.mark(v.tensor_tensor(tmp[t % 2][:, :], y, bias, ALU.add))
                        ch.need(n)
                        n = ch.mark(v.tensor_tensor(tmp[t % 2][:, :], tmp[t % 2][:, :], gate_row, ALU.mult))
                        ch.need(n)
                        y = tmp[t % 2][:, :]
                    v.tensor_tensor(dst[:, t, :], dst[:, t, :], y, ALU.add).then_inc(s["x"], 1)
                v.wait_ge(s["x"], b * NT + NT)

            with v.Fori(0, B) as b:
                v.wait_ge(s_bld, b * 128 + 128)
                norm("n0", b, X)
                attention(A0, b)
                project(A0, b, X, bo_bc[:, 0, :], bc[:, 0, :])
                norm("n1", b, X)
                for t in range(NT):
                    v.wait_ge(f0["lg"], b * NT + t + 1)
                    v.tensor_tensor(lg[:, t, :], pT[t % 2][:, 0:D], bg_bc[:, :], ALU.add).then_inc(f0["le"], 1)
                second = ch.n
                v.wait_ge(f0["le"], b * NT + NT)
                v.memset(ixf[:, :, :], 0.0)
                for t in range(NT):
                    ch.mark(v.max(v8[:, t, :], lg[:, t, :]))
                for t in range(NT):
                    ch.need(second + t + 1)
                    ch.mark(v.max_index(ix8[:, t, :], v8[:, t, :], lg[:, t, :]))
                ch.need(ch.n)
                v.tensor_scalar(gsm[:, :, 0], v8[:, :, 0], -1.0, None, ALU.mult).then_inc(f0["nm"], 1)
                n = ch.mark(v.tensor_scalar(ix8[:, :, 1], ix8[:, :, 0], E - 1, None, ALU.bitwise_and))
                ch.need(n)
                n = ch.mark(v.tensor_copy(ixf[:, :, 0], ix8[:, :, 1]))
                ch.need(n)
                iota_bc = iota8[:, :].unsqueeze(1).to_broadcast([P, NT, E])
                n = ch.mark(v.tensor_tensor(gate[:, :, :], iota_bc, ixf[:, :, 0:1].to_broadcast([P, NT, E]),
                                            ALU.is_equal))
                v.wait_ge(f0["se"], b * NT + NT)
                n = ch.mark(v.reciprocal(gsm[:, :, 2], gsm[:, :, 1]))
                ch.need(n)
                m = v.tensor_tensor(gate[:, :, :], gate[:, :, :], gsm[:, :, 2:3].to_broadcast([P, NT, E]), ALU.mult)
                m.then_inc(f0["g"], 1)
                v.wait_ge(f0["gt"], b + 1)
                for h in range(2):
                    v.tensor_copy(gT[:, h * 512:h * 512 + 512], pT[h][0:E, :]).then_inc(f0["ge"], 1)
                for t in range(NT):
                    made = [0, 0]
                    for e in range(E):
                        c = e % 2
                        src = pA[e // 4][:, e % 4 * D:e % 4 * D + D]
                        if e % 4 == 0:
                            v.wait_ge(f0["y"], b * 2 * NT + 2 * t + e // 4 + 1)
                        if e < 2:
                            m = v.tensor_scalar(acc[c], src, gate[:, t, e:e + 1], None, ALU.mult)
                        else:
                            if made[c] is None:
                                v.wait_ge(f0["yc"], b * 2 * NT + 2 * t + 1)
                            else:
                                ch.need(made[c])
                            m = v.scalar_tensor_tensor(out=acc[c], in0=src, scalar=gate[:, t, e:e + 1],
                                                       in1=acc[c], op0=ALU.mult, op1=ALU.add)
                        if e % 4 == 3:
                            m.then_inc(f0["yc"], 1)
                            made[c] = None
                        else:
                            made[c] = ch.mark(m)
                    ch.need(made[0])
                    v.wait_ge(f0["yc"], b * 2 * NT + 2 * t + 2)
                    n = ch.mark(v.tensor_tensor(acc[2], acc[0], acc[1], ALU.add))
                    v.wait_ge(f0["yb"], b * NT + t + 1)
                    ch.need(n)
                    n = ch.mark(v.tensor_tensor(acc[3], acc[2], pT[t % 2][:, 0:D], ALU.add))
                    ch.need(n)
                    n = ch.mark(v.scalar_tensor_tensor(out=tmp[0][:, :], in0=acc[3], scalar=0.0, in1=bc[:, 1, :],
                                                       op0=ALU.max, op1=ALU.mult))
                    ch.need(n)
                    m = v.tensor_tensor(X[:, t, :], X[:, t, :], tmp[0][:, :], ALU.add)
                    m.then_inc(f0["x"], 1)
                v.wait_ge(f0["x"], b * NT + NT)
                norm("n2", b, X)
                attention(A1, b)
                project(A1, b, X, bo_bc[:, 1, :], bc[:, 2, :])
                norm("n3", b, X)
                v.wait_ge(ln["n3"]["xn"], b * NT + NT)
                for t in range(NT):
                    n = ch.mark(v.tensor_tensor(Z[:, t, :], xn[:, t, :], bc[:, 4, :], ALU.mult))
                ch.need(n)
                for t in range(NT):
                    n = ch.mark(v.tensor_tensor(Z[:, t, :], Z[:, t, :], bc[:, 3, :], ALU.add))
                ch.need(n)
                norm("n4", b, Z)
                attention(A2, b)
                project(A2, b, Z, None, None)
                norm("n5", b, Z)
                v.wait_ge(m1["lg"], b + 1)
                n = ch.mark(v.tensor_copy(gate2[:, :, :], pT[0][:, 0:NT * E].rearrange("p (t e) -> p t e", e=E)))
                ch.need(n)
                for t in range(NT):
                    n = ch.mark(v.max(v8[:, t, :], gate2[:, t, :]))
                ch.need(n)
                v.tensor_tensor(gsm[:, :, 0], v8[:, :, 1], v8[:, :, 0], ALU.subtract).then_inc(m1["df"], 1)
                for t in range(NT):
                    n = ch.mark(v.max_index(ix8[:, t, :], v8[:, t, :], gate2[:, t, :]))
                ch.need(n)
                n = ch.mark(v.tensor_copy(ixf[:, :, :], ix8[:, :, 0:2]))
                v.wait_ge(m1["e1"], b + 1)
                n = ch.mark(v.tensor_scalar(gsm[:, :, 2], gsm[:, :, 1], 1.0, None, ALU.add))
                ch.need(n)
                n = ch.mark(v.reciprocal(gsm[:, :, 3], gsm[:, :, 2]))
                ch.need(n)
                n = ch.mark(v.tensor_tensor(gsm[:, :, 4], gsm[:, :, 1], gsm[:, :, 3], ALU.mult))
                for r, dst in ((0, gate), (1, gate2)):
                    n = ch.mark(v.tensor_tensor(dst[:, :, :], iota_bc, ixf[:, :, r:r + 1].to_broadcast([P, NT, E]),
                                                ALU.is_equal))
                ch.need(n)
                for r, dst in ((0, gate), (1, gate2)):
                    n = ch.mark(v.tensor_tensor(dst[:, :, :], dst[:, :, :],
                                                gsm[:, :, 3 + r:4 + r].to_broadcast([P, NT, E]), ALU.mult))
                ch.need(n)
                m = v.tensor_tensor(gate[:, :, :], gate[:, :, :], gate2[:, :, :], ALU.add)
                m.then_inc(m1["g"], 1)
                ch.restart()
                with v.Fori(0, E // 2) as ep:
                    it = b * (E // 2) + ep
                    for q in range(2 * NT):
                        par, t = q // NT, q % NT
                        v.wait_ge(m1["y"], it * 2 * NT + q + 1)
                        v.wait_ge(m1["z"], it * 2 * NT + max(q - NT + 1, 0))
                        v.scalar_tensor_tensor(out=Z[:, t, :], in0=pT[q % 2][:, 0:D],
                                               scalar=gate[:, t, bass.ds(ep * 2 + par, 1)], in1=Z[:, t, :],
                                               op0=ALU.mult, op1=ALU.add).then_inc(m1["z"], 1)
                v.wait_ge(m1["z"], b * E * NT + E * NT)
                for t in range(NT):
                    n = ch.mark(v.tensor_tensor(Z[:, t, :], Z[:, t, :], bc[:, 5, :], ALU.mult))
                ch.need(n)
                for t in range(NT):
                    n = ch.mark(v.tensor_tensor(X[:, t, :], X[:, t, :], Z[:, t, :], ALU.add))
                ch.need(n)
                v.sem_inc(s_fin, 1)
                ch.restart()


_INS = ["x", "ct", "wmod0", "wmod1", "wqkv0", "wqkv1", "wqkv2", "bqk0", "bqk1", "bv0", "bv1", "wo0", "wo1", "wo2",
        "bo0", "bo1", "ffn_wg", "ffn_bg", "ffn_we", "ffn_be", "ln_w", "router_w", "w1", "w2"]


def kernel(**inp):
    import numpy as np
    import concourse.bacc as _bacc
    from concourse.bass_utils import run_bass_kernel_spmd as _run

    def slots(w, slot):
        w = np.asarray(w)
        d = w.shape[-1] // 16
        w = w.reshape(w.shape[:-1] + (16, d))
        if d < slot:
            pad = np.zeros(w.shape[:-1] + (slot - d,), w.dtype)
            w = np.concatenate([w, pad], axis=-1)
        return w.reshape(w.shape[:-2] + (16 * slot // P, P))

    def group(wq, wk, wv, slot):
        ws = [slots(w, slot).reshape(KC, P, -1, P).transpose(2, 1, 0, 3) for w in (wq, wk, wv)]
        return np.ascontiguousarray(np.concatenate(ws, axis=3))

    def out_weights(w, slot):
        return np.ascontiguousarray(slots(np.asarray(w).T, slot).transpose(2, 1, 0))

    a = {k: np.asarray(v) for k, v in inp.items()}
    qkv = a["L1_attn_W_qkv"].reshape(D, 3, N)
    bqkv = a["L1_attn_b_qkv"].reshape(3, N)
    cat = a["L1_ffn_c_attn_w"].reshape(D, 3, D)
    arr = {
        "x": a["L0_attn_x"],
        "ct": np.ascontiguousarray(np.stack([a["L0_c"], a["L1_c"]]).reshape(2, B, KC, P).transpose(3, 0, 2, 1)),
        "wmod0": a["L0_wmod"], "wmod1": a["L1_wmod"],
        "wqkv0": group(a["L0_attn_Wq"].T, a["L0_attn_Wk"].T, a["L0_attn_Wv"].T, 32),
        "wqkv1": group(qkv[:, 0], qkv[:, 1], qkv[:, 2], 64),
        "wqkv2": group(cat[:, 0], cat[:, 1], cat[:, 2], 32),
        "bqk0": np.ascontiguousarray(np.stack([slots(a["L0_attn_bq"], 32), slots(a["L0_attn_bk"], 32)], axis=2)),
        "bqk1": np.ascontiguousarray(np.stack([slots(bqkv[0], 64), slots(bqkv[1], 64)], axis=2)),
        "bv0": np.ascontiguousarray(slots(a["L0_attn_bv"], 32)),
        "bv1": np.ascontiguousarray(slots(bqkv[2], 64)),
        "wo0": out_weights(a["L0_attn_Wo"].T, 32),
        "wo1": out_weights(a["L1_attn_W_out"], 64),
        "wo2": out_weights(a["L1_ffn_c_proj_w"], 32),
        "bo0": a["L0_attn_bo"], "bo1": a["L1_attn_b_out"],
        "ffn_wg": a["L0_ffn_Wg"], "ffn_bg": a["L0_ffn_bg"], "ffn_we": np.ascontiguousarray(a["L0_ffn_We"].reshape(E, KC, P, D).transpose(2, 1, 0, 3)),
         "ffn_be": a["L0_ffn_be"],
        "ln_w": np.ascontiguousarray(np.stack([a["L1_ffn_ln1_w"], a["L1_ffn_ln2_w"]]).reshape(2, KC, P)
                                     .transpose(2, 0, 1)),
        "router_w": a["L1_ffn_router_w"],
        "w1": np.ascontiguousarray(a["L1_ffn_w1"].reshape(KC, P, E, F).transpose(2, 1, 0, 3)),
        "w2": np.ascontiguousarray(a["L1_ffn_w2"].reshape(E, FC, P, D).transpose(0, 2, 1, 3)),
    }
    nc = _bacc.Bacc("TRN2", target_bir_lowering=False, num_devices=1)
    ap, arrays = {}, {}
    for name in _INS:
        arrays[f"in_{name}"] = np.ascontiguousarray(arr[name])
        ap[name] = nc.dram_tensor(f"in_{name}", arr[name].shape, F32, kind="ExternalInput").ap()
    out = nc.dram_tensor("out_0", (B, N, D), F32, kind="ExternalOutput").ap()
    build(nc, ap["x"], ap["ct"], [ap["wmod0"], ap["wmod1"]], [ap["wqkv0"], ap["wqkv1"], ap["wqkv2"]],
          [ap["bqk0"], ap["bqk1"]], [ap["bv0"], ap["bv1"]], [ap["wo0"], ap["wo1"], ap["wo2"]],
          [ap["bo0"], ap["bo1"]], ap["ffn_wg"], ap["ffn_bg"], ap["ffn_we"], ap["ffn_be"], ap["ln_w"],
          ap["router_w"], ap["w1"], ap["w2"], out)
    r = _run(nc, [arrays], core_ids=[0])
    return r.results[0]["out_0"]
```

```python
from contextlib import ExitStack

import concourse.bass as bass
from concourse import mybir

F32 = mybir.dt.float32
BF16 = mybir.dt.bfloat16
U32 = mybir.dt.uint32
ALU = mybir.AluOpType
ACT = mybir.ActivationFunctionType
AX = mybir.AxisListType.X

P = 128
B = 4
N = 1024
D = 256
NT = N // P
KC = D // P
EPS = 1e-5
TOPK = 32
E = 8
F = 512
FC = F // P
NEG_REPLACED = -3.0e38


class Attn:

    def __init__(self, name, slot, head, topk, bias, mask):
        self.name, self.slot, self.topk, self.bias = name, slot, topk, bias
        self.hg = P // slot
        self.groups = 16 // self.hg
        self.scale = float(head) ** -0.5
        self.mask = mask
        self.narrow = head == 16
        self.units = NT * self.hg
        self.pairs = self.units // 2
        self.chunks = [(i // 4 + 1) for i in range(NT) for _ in range(self.hg)]
        self.chunk_at = [sum(self.chunks[:u]) for u in range(self.units + 1)]

    def unit(self, u):
        return u // self.hg, u % self.hg


A0 = Attn("a0", 32, 16, True, True, 0)
A1 = Attn("a1", 64, 64, False, True, 1)
A2 = Attn("a2", 32, 16, False, False, 0)
LNS = ["n0", "n1", "n2", "n3", "n4", "n5"]


class Chain:

    def __init__(self, eng, sem):
        self.eng, self.sem, self.n = eng, sem, 0

    def mark(self, ins):
        ins.then_inc(self.sem, 1)
        self.n += 1
        return self.n

    def need(self, n):
        self.eng.wait_ge(self.sem, n)

    def restart(self):
        self.eng.wait_ge(self.sem, self.n)
        self.eng.sem_clear(self.sem)
        self.n = 0


def build(nc, x, ct, wmod, wqkv, bqk, bv, wo, bo, ffn_wg, ffn_bg, ffn_we, ffn_be, ln_w, router_w, w1, w2, out):
    ctx = ExitStack()
    with ctx:
        def sb(name, shape, dt=F32):
            return ctx.enter_context(nc.sbuf_tensor(name, shape, dt))

        def ps(name, shape, dt=F32):
            return ctx.enter_context(nc.psum_tensor(name, shape, dt))

        def sem(name):
            return ctx.enter_context(nc.semaphore(name))

        mod_dram = nc.dram_tensor("mod_rows", (B, 2, 6, D), F32, kind="Internal").ap()

        pA = [ps(f"pA{i}", [P, N]) for i in range(2)]
        pT = [ps(f"pT{i}", [P, 512]) for i in range(2)]
        pO = ps("pO", [P, N])

        ident = sb("ident", [P, P])
        identm = sb("identm", [P, P], BF16)
        tri = sb("tri", [P, 2, P], BF16)
        iota8 = sb("iota8", [P, E])
        mhalf = sb("mhalf", [P, NT])
        ctile = sb("ctile", [P, 2, KC, B])
        csig = sb("csig", [P, 2, KC, B])
        wg = sb("wg", [P, KC, D])
        bg_bc = sb("bg_bc", [P, D])
        be = sb("be", [E, D])
        lnw = sb("lnw", [P, 2, KC])
        rw = sb("rw", [P, KC, E])
        bo_bc = sb("bo_bc", [P, 2, D])

        X = sb("X", [P, NT, D])
        Z = sb("Z", [P, NT, D])
        hT = sb("hT", [P, KC, N])
        fmr = sb("fmr", [P, P])
        fm = sb("fm", [P, 2, 6, KC])
        bc = sb("bc", [P, 6, D])
        st = sb("st", [P, NT, 6])
        mv = sb("mv", [P, NT, 2])
        ve = sb("ve", [P, NT])
        rstd = sb("rstd", [P, NT])

        bqk_sb = sb("bqk_sb", [P, 2])
        bq_s = sb("bq_s", [P, 1])
        bv_bc = sb("bv_bc", [P, P])
        stack = sb("stack", [P, 2, 16, N], BF16)
        bqk_n = sb("bqk_n", [P, 2, KC])
        bq_n = sb("bq_n", [P, KC])
        wo_sb = sb("wo_sb", [P, 8, D])
        bv_n = sb("bv_n", [P, 4 * P])
        vs = sb("vs", [P, NT, P])
        oall_n = sb("oall_n", [P, 4, N])
        vall = oall_n[:, :, :].rearrange("p g (t d) -> p g t d", d=P)
        first_half = stack[:, 0, :, :].rearrange("p h n -> p (h n)").bitcast(F32)
        we = first_half[:, 0:4096].rearrange("p (k e n) -> p k e n", k=KC, e=E)
        qm = first_half[:, 4096:4096 + 2 * N].rearrange("p (j n) -> p j n", j=2)
        kT = first_half[:, 6144:6144 + N]
        wq = first_half[:, 7168:7168 + KC * 3 * P].rearrange("p (k n) -> p k n", k=KC)
        oall_w = stack[:, 1, :, :].rearrange("p h n -> p (h n)").bitcast(F32).rearrange("p (g n) -> p g n", g=8)
        ssb = sb("ssb", [P, 4, N])
        work = sb("work", [P, 2, N])
        pr = sb("pr", [P, 4, N])
        prT = sb("prT", [P, 4, N])
        keep = sb("keep", [P, 2, N], BF16)
        junk = sb("junk", [P, 2, N], BF16)
        thr = sb("thr", [P, 2])
        ones2 = sb("ones2", [P, 2])
        step = sb("step", [P, 2])
        vals = sb("vals", [P, 4, TOPK])
        nmax = sb("nmax", [P, 4])
        rsum = sb("rsum", [P, 32])
        rinv = sb("rinv", [P, 32])
        rbc = work[:, 0, :]
        xn = work[:, :, :].rearrange("p a (t d) -> p (a t) d", d=D)
        wqn = prT[:, :, :].rearrange("p a n -> p (a n)")[:, 0:KC * N].rearrange("p (k n) -> p k n", k=KC)
        full = ssb
        part = pr[:, :, :].rearrange("p a n -> p (a n)").bitcast(BF16).rearrange("p (x n) -> p x n", n=N)
        lowp = work[:, :, :].rearrange("p a n -> p (a n)").bitcast(BF16).rearrange("p (x n) -> p x n", n=N)

        lg = ssb[:, 0:2, :].rearrange("p a (t d) -> p (a t) d", d=D)
        v8 = sb("v8", [P, NT, 8])
        ix8 = sb("ix8", [P, NT, 8], U32)
        ixf = sb("ixf", [P, NT, 2])
        gsm = sb("gsm", [P, NT, 8])
        gate = sb("gate", [P, NT, E])
        gate2 = sb("gate2", [P, NT, E])
        gT = sb("gT", [E, N])
        acc = [work[:, 1, i * D:(i + 1) * D] for i in range(4)]
        tmp = [sb(f"tmp{i}", [P, D]) for i in range(2)]
        H = [pr[:, 2 * i:2 * i + 2, :].rearrange("p a (f n) -> p (a f) n", n=512) for i in range(2)]
        w1_sb = [ssb[:, i, :].rearrange("p (k f) -> p k f", k=KC) for i in range(2)]
        w2_sb = [ssb[:, 2 + i, :].rearrange("p (k f) -> p k f", k=FC) for i in range(2)]
        wm_sb = [oall_w[:, 3 * i:3 * i + 3, :].rearrange("p a n -> p (a n)").rearrange("p (k n) -> p k n", k=KC)
                 for i in range(2)]
        modrow = oall_w[0:B, 6:8, :].rearrange("p a n -> p (a n)")[:, 0:6 * D]
        modtmp = ssb[0:B, 0, 0:D]
        modsgn = ssb[0:B, 1, 0:D]

        s_const = sem("s_const")
        s_wld = sem("s_wld")
        s_mld = sem("s_mld")
        s_cexp = sem("s_cexp")
        s_csil = sem("s_csil")
        s_mmm = sem("s_mmm")
        s_mrow = sem("s_mrow")
        s_mst = sem("s_mst")
        s_bld = sem("s_bld")
        s_fmt = sem("s_fmt")
        s_fm = sem("s_fm")
        s_fin = sem("s_fin")
        s_out = sem("s_out")
        s_qz = sem("s_qz")
        dv = sem("dv")
        ac = sem("ac")
        ln = {}
        for n in LNS:
            ln[n] = {k: sem(f"{n}_{k}") for k in (
                "var",
                "rs",
                "xn",
                "tr",
                "ev",
            )}
        only = {"narrow": ("wn", "pn", "fn", "hn", "rn", "st", "vn", "vw", "vg"), "wide": ("w", "eqk", "ev"),
                "topk": ("cp", "th", "k", "p", "rs"), "plain": (), "bias": ("bs",)}
        at = {}
        for a in (A0, A1, A2):
            without = only["wide" if a.narrow else "narrow"] + (() if a.topk else only["topk"])\
                + (() if a.bias else only["bias"])
            at[a.name] = {k: sem(f"{a.name}_{k}") for k in (
                "w",
                "wo",
                "pj",
                "bs",
                "eqk",
                "ev",
                "s",
                "cp",
                "mx",
                "e",
                "wn",
                "pn",
                "fn",
                "hn",
                "rn",
                "st",
                "vn",
                "vw",
                "vg",
                "th",
                "k",
                "p",
                "rs",
                "t",
                "te",
                "te2",
                "pv",
                "ri",
                "bc",
                "be",
                "o",
                "y",
                "x",
            ) if k not in without}
        f0 = {k: sem(f"f0_{k}") for k in (
            "w",
            "lg",
            "le",
            "nm",
            "se",
            "g",
            "gt",
            "ge",
            "y",
            "yb",
            "yc",
            "x",
        )}
        m1 = {k: sem(f"m1_{k}") for k in (
            "w0",
            "w1",
            "lg",
            "df",
            "e1",
            "g",
            "h",
            "ge",
            "y",
            "z",
        )}

        N_WLD = 16 * 9
        TERMS = ((0, 0), (0, 1), (1, 0), (0, 2), (2, 0), (1, 1))
        KROWS = 16 * len(TERMS)
        gw_d = {a.name: wqkv[n] for n, a in enumerate((A0, A1, A2))}
        block = ctx.enter_context(nc.Block())

        @block.sync
        def _(sp):
            sp.dma_start(ctile[:, :, :, :], ct).then_inc(s_mld, 16)
            for l in range(2):
                sp.dma_start(wm_sb[l], wmod[l].rearrange("(k p) n -> p k n", p=P)).then_inc(s_mld, 16)
            for dst, src in (
                (wg[:, :, :], ffn_wg.rearrange("(k p) n -> p k n", p=P)),
                (bg_bc[:, :], ffn_bg.partition_broadcast(P)),
                (be[:, :], ffn_be),
                (bqk_n[:, :, :], bqk[0]),
                (bv_n[:, :], bv[0].partition_broadcast(P)),
                (lnw[:, :, :], ln_w),
                (rw[:, :, :], router_w.rearrange("(k p) n -> p k n", p=P)),
                (bo_bc[:, 0, :], bo[0].partition_broadcast(P)),
                (bo_bc[:, 1, :], bo[1].partition_broadcast(P)),
            ):
                sp.dma_start(dst, src).then_inc(s_wld, 16)
            for l in range(2):
                sp.wait_ge(s_mrow, l + 1)
                sp.dma_start(mod_dram[:, l],
                             modrow.rearrange("b (j d) -> b j d", j=6)).then_inc(s_mst, 16)
            sp.wait_ge(s_mst, 32)

            def group_weights(a, g):
                s = at[a.name]
                sp.dma_start(wq, gw_d[a.name][bass.ds(g, 1)].rearrange("a p k n -> (a p) k n"))\
                  .then_inc(s["w"], 16)
                if a.bias:
                    sp.dma_start(bqk_sb[:, :], bqk[1][bass.ds(g, 1)].rearrange("a p n -> (a p) n"))\
                      .then_inc(s["w"], 16)
                    sp.dma_start(bv_bc[:, :], bv[1][bass.ds(g, 1)].partition_broadcast(P)
                                 .rearrange("p a n -> p (a n)")).then_inc(s["w"], 16)

            with sp.Fori(0, B) as b:
                sp.wait_ge(s_out, b * 16)
                sp.dma_start(X[:, :, :], x[bass.ds(b, 1)].rearrange("a (t p) d -> p (a t) d", p=P))\
                  .then_inc(s_bld, 16)
                sp.dma_start(fmr[0:24, :], mod_dram[bass.ds(b, 1)]
                             .rearrange("a l j (c p) -> (a l j c) p", p=P)).then_inc(s_bld, 16)
                for i, (l, j) in enumerate(((0, 2), (0, 5), (1, 2), (1, 3), (1, 4), (1, 5))):
                    sp.dma_start(bc[:, i, :], mod_dram[bass.ds(b, 1), l, j, :].partition_broadcast(P)
                                 .rearrange("p a n -> p (a n)")).then_inc(s_bld, 16)
                prev = None
                for n, a in enumerate((A0, A1, A2)):
                    if prev is not None:
                        sp.wait_ge(at[prev.name]["y"], b * NT + NT)
                    sp.dma_start(wo_sb[:, 0:a.groups, :], wo[n]).then_inc(at[a.name]["wo"], 16)
                    if a.narrow:
                        s = at[a.name]
                        sp.dma_start(wqn, wqkv[n]).then_inc(s["wn"], 16)
                        for c in range(KC):
                            sp.wait_ge(s["rn"], (b * KC + c + 1) * 4)
                            sp.wait_ge(s["hn"], (b * KC + c + 1) * 4)
                            for side in range(2):
                                for t, term in enumerate(TERMS):
                                    q = 2 * c + side
                                    src = lowp[:, q, :] if term[side] == 2 else part[:, 2 * q + term[side], :]
                                    sp.dma_start(stack[16 * t:16 * t + 16, side, 8 * c:8 * c + 8, :],
                                                 src).then_inc(s["st"], 16)
                    else:
                        group_weights(a, 0)
                        with sp.Fori(0, a.groups - 1) as g:
                            sp.wait_ge(at[a.name]["s"], (b * a.groups + g) * a.units + 1)
                            group_weights(a, g + 1)
                    if a is A0:
                        sp.wait_ge(at["a0"]["y"], b * NT + NT)
                        sp.dma_start(we, ffn_we).then_inc(f0["w"], 16)
                    prev = a
                sp.wait_ge(m1["df"], b + 1)

                def expert(par, e):
                    sp.dma_start(w1_sb[par], w1[bass.ds(e, 1)].rearrange("a p k n -> (a p) k n"))\
                      .then_inc(m1["w%d" % par], 16)
                    sp.dma_start(w2_sb[par], w2[bass.ds(e, 1)].rearrange("a p k n -> (a p) k n"))\
                      .then_inc(m1["w%d" % par], 16)

                expert(0, 0)
                with sp.Fori(0, E // 2 - 1) as ep:
                    it = b * (E // 2) + ep
                    sp.wait_ge(m1["y"], it * 2 * NT)
                    expert(1, ep * 2 + 1)
                    sp.wait_ge(m1["y"], it * 2 * NT + NT)
                    expert(0, ep * 2 + 2)
                sp.wait_ge(m1["y"], (b * (E // 2) + E // 2 - 1) * 2 * NT)
                expert(1, E - 1)
                sp.wait_ge(s_fin, b + 1)
                sp.dma_start(out[bass.ds(b, 1)].rearrange("a (t p) d -> p (a t) d", p=P), X[:, :, :])\
                  .then_inc(s_out, 16)
            sp.wait_ge(s_out, B * 16)

        @block.gpsimd
        def _(pool):
            c = Chain(pool, s_const)
            c.mark(pool.memset(ident[:, :], 0.0))
            c.mark(pool.memset(identm[:, :], 0.0))
            c.mark(pool.memset(tri[:, :, :], 0.0))
            c.mark(pool.memset(mhalf[:, :], -0.5))
            c.mark(pool.memset(fmr[:, :], 0.0))
            c.mark(pool.memset(ones2[:, :], 1.0))
            c.mark(pool.iota(iota8[:, :], pattern=[[1, E]], base=0, channel_multiplier=0,
                             allow_small_or_imprecise_dtypes=True))
            c.need(c.n)
            c.mark(pool.affine_select(out=ident[:, :], in_=ident[:, :], compare_op=ALU.not_equal, fill=1.0,
                                      base=0, pattern=[[-1, P]], channel_multiplier=1))
            c.mark(pool.affine_select(out=identm[:, :], in_=identm[:, :], compare_op=ALU.not_equal, fill=80.0,
                                      base=0, pattern=[[-1, P]], channel_multiplier=1))
            for m, value in ((0, -(2.0 ** 90)), (1, -125.0)):
                c.mark(pool.affine_select(out=tri[:, m, :], in_=tri[:, m, :], compare_op=ALU.is_ge, fill=value,
                                          base=0, pattern=[[-1, P]], channel_multiplier=1))

            def norm(n, b):
                pool.wait_ge(ln[n]["var"], b + 1)
                pool.tensor_tensor(rstd[:, :], ve[:, :], mhalf[:, :], ALU.pow).then_inc(ln[n]["rs"], 1)

            def narrow(a, b):
                s = at[a.name]
                U, CH = a.units, a.chunk_at[-1]
                with pool.Fori(0, a.groups) as g:
                    it = b * a.groups + g
                    steps = 1 + (a.pairs if a.topk else 0)

                    pool.wait_ge(s["vn"], b * 4 + 4)
                    pool.wait_ge(s["pv"], it * a.pairs)
                    pool.wait_ge(s["vw"], it * steps)
                    pool.tensor_tensor(thr[:, :], ones2[:, :], ones2[:, :], ALU.mult).then_inc(s["vw"], 1)
                    pool.tensor_copy(vs[:, :, :], vall[:, bass.ds(g, 1), :, :].rearrange("p a t d -> p (a t) d")).then_inc(s["vg"], 1)
                    if a.topk:
                        def select(p):
                            us = (2 * p, 2 * p + 1)
                            w = (a.unit(us[0])[0] + 1) * P
                            pool.wait_ge(s["th"], it * U + 2 * p + 2)
                            pool.wait_ge(s["p"], it * U + 2 * p)
                            pool.wait_ge(s["vw"], it * steps + 1 + p)
                            pool.tensor_tensor(thr[:, :], vals[:, us[0] % 4:us[0] % 4 + 2, TOPK - 1], ones2[:, :],
                                               ALU.mult).then_inc(s["vw"], 1)
                            for u in us:
                                pool.tensor_scalar(keep[:, u % 2, 0:w], ssb[:, u % 4, 0:w],
                                                   vals[:, u % 4, TOPK - 1:TOPK], None, ALU.is_ge)\
                                    .then_inc(s["k"], 1)
                            for u in us:
                                pool.wait_ge(s["k"], it * U + u + 1)
                                pool.wait_ge(s["e"], it * U + u + 1)
                                pool.tensor_tensor(pr[:, u % 4, 0:w], keep[:, u % 2, 0:w], pr[:, u % 4, 0:w],
                                                   ALU.mult).then_inc(s["p"], 1)
                        for p in range(a.pairs):
                            select(p)

            with pool.Fori(0, B) as b:
                norm("n0", b)
                narrow(A0, b)
                norm("n1", b)
                pool.memset(qm, 0.0).then_inc(s_qz, 1)
                for n in LNS[2:5]:
                    norm(n, b)
                narrow(A2, b)
                norm("n5", b)
        N_CONST = 11

        @block.scalar
        def _(act):
            chain = Chain(act, ac)
            act.wait_ge(s_mld, 48)
            act.activation(csig[:, :, :, :], ctile[:, :, :, :], ACT.Exp, scale=-1.0).then_inc(s_cexp, 1)
            act.wait_ge(s_wld, N_WLD)

            def norm(n, b, scale, shift):
                s = ln[n]
                for idx in range(4):
                    half, c = idx // 2, idx % 2
                    act.wait_ge(s["tr"], b * 4 + idx + 1)
                    act.activation(hT[:, c, half * 512:half * 512 + 512], pT[idx % 2][:, :], ACT.Identity,
                                   scale=scale[:, c:c + 1],
                                   bias=shift[:, c:c + 1] if shift is not None else 0.0).then_inc(s["ev"], 1)

            def project_narrow(a, b):
                s = at[a.name]
                if a.bias:
                    act.mul(bq_n[:, :], bqk_n[:, 0, :], a.scale).then_inc(s["bs"], 1)
                    act.wait_ge(s["bs"], b + 1)
                for c in range(KC):
                    for x in range(2):
                        q = 2 * c + x
                        act.wait_ge(s["pn"], b * 4 + q + 1)
                        bias = (bq_n if x == 0 else bqk_n[:, 1, :])[:, c:c + 1] if a.bias else 0.0
                        act.activation(full[:, q, :], pA[x][:, :], ACT.Identity, scale=a.scale if x == 0 else 1.0,
                                       bias=bias).then_inc(s["fn"], 1)
                    for x in range(2):
                        q = 2 * c + x
                        act.wait_ge(s["fn"], b * 4 + q + 1)
                        act.activation(part[:, 4 * c + 2 * x, :], full[:, q, :], ACT.Copy).then_inc(s["hn"], 1)
                    for x in range(2):
                        q = 2 * c + x
                        act.wait_ge(s["rn"], b * 8 + 4 * c + x + 1)
                        act.activation(part[:, 4 * c + 2 * x + 1, :], full[:, q, :], ACT.Copy).then_inc(s["hn"], 1)

            def attention(a, b):
                s = at[a.name]
                U, CH = a.units, a.chunk_at[-1]
                nw = 48 if a.bias else 16
                if a.narrow:
                    project_narrow(a, b)
                with act.Fori(0, a.groups) as g:
                    it = b * a.groups + g
                    if not a.narrow:
                        act.wait_ge(s["w"], it * nw + nw)
                        act.mul(bq_s[:, :], bqk_sb[:, 0:1], a.scale).then_inc(s["bs"], 1)
                        act.wait_ge(s["bs"], it + 1)
                        act.wait_ge(s_qz, b + 1)
                        act.wait_ge(s["pj"], it * 3 + 1)
                        for j in range(a.hg):
                            sl = slice(j * a.slot, (j + 1) * a.slot)
                            act.activation(qm[sl, j, :], pA[0][sl, :], ACT.Identity, scale=a.scale,
                                           bias=bq_s[sl, :]).then_inc(s["eqk"], 1)
                        act.wait_ge(s["pj"], it * 3 + 2)
                        act.activation(kT, pA[1][:, :], ACT.Identity, bias=bqk_sb[:, 1:2])\
                           .then_inc(s["eqk"], 1)

                    def copy(u):
                        i, j = a.unit(u)
                        w = (i + 1) * P
                        act.wait_ge(s["s"], it * U + u + 1)
                        act.wait_ge(s["p"], it * U + max(u - 3, 0))
                        act.activation(ssb[:, u % 4, 0:w], pA[u % 2][:, 0:w], ACT.Copy).then_inc(s["cp"], 1)

                    def exp_topk(u):
                        i, j = a.unit(u)
                        w = (i + 1) * P
                        act.wait_ge(s["mx"], it * a.pairs + u // 2 + 1)
                        act.wait_ge(s["t"], it * CH + a.chunk_at[max(u - 3, 0)])
                        act.activation(pr[:, u % 4, 0:w], ssb[:, u % 4, 0:w], ACT.Exp,
                                       bias=nmax[:, u % 4:u % 4 + 1]).then_inc(s["e"], 1)

                    def exp_plain(u):
                        i, j = a.unit(u)
                        w = (i + 1) * P
                        act.wait_ge(s["s"], it * U + u + 1)
                        act.wait_ge(s["mx"], it * U + u + 1)
                        act.wait_ge(s["t"], it * CH + a.chunk_at[max(u - 3, 0)])
                        act.activation(pr[:, u % 4, 0:w], pA[u % 2][:, 0:w], ACT.Exp,
                                       bias=nmax[:, u % 4:u % 4 + 1],
                                       accum_out=rsum[:, u:u + 1]).then_inc(s["e"], 1)

                    def out_of_psum(u, first):
                        i, j = a.unit(u)
                        for c in range(first, a.chunks[u]):
                            q = a.chunk_at[u] + c
                            w = min(i + 1 - 4 * c, 4) * P
                            act.wait_ge(s["t"], it * CH + q + 1)
                            act.wait_ge(s["pv"], it * a.pairs + max(u // 2 - 1, 0))
                            act.activation(prT[:, u % 4, c * 512:c * 512 + w], pT[q % 2][:, 0:w], ACT.Copy)\
                               .then_inc(s["te"] if c == 0 else s["te2"], 1)

                    def row_sum(u):
                        w = (a.unit(u)[0] + 1) * P
                        act.wait_ge(s["p"], it * U + u + 1)
                        act.wait_ge(s["rs"], it * U + max(u - 1, 0))
                        act.activation(junk[:, u % 2, 0:w], pr[:, u % 4, 0:w], ACT.Copy,
                                       accum_out=rsum[:, u:u + 1]).then_inc(s["rs"], 1)

                    if a.topk:
                        for u in range(4):
                            copy(u)
                        for p in range(a.pairs):
                            for u in (2 * p, 2 * p + 1):
                                exp_topk(u)
                            if p >= 1:
                                for u in (2 * p - 2, 2 * p - 1):
                                    row_sum(u)
                                    if u + 4 < U:
                                        copy(u + 4)
                                    out_of_psum(u, 0)
                        for u in (U - 2, U - 1):
                            row_sum(u)
                            out_of_psum(u, 0)
                    else:
                        for u in range(U):
                            exp_plain(u)
                            if u >= 1:
                                out_of_psum(u - 1, 1)
                        out_of_psum(U - 1, 1)
                    act.wait_ge(s["bc"], it + 1)
                    act.wait_ge(s["o"], it)
                    act.activation(rbc, pA[0][:, :], ACT.Copy).then_inc(s["be"], 1)

            with act.Fori(0, B) as b:
                act.wait_ge(s_fmt, b + 1)
                act.activation(fm[:, :, :, :].rearrange("p l j c -> p (l j c)"), pT[0][:, 0:24], ACT.Copy)\
                   .then_inc(s_fm, 1)
                act.wait_ge(s_fm, b + 1)
                norm("n0", b, fm[:, 0, 1, :], fm[:, 0, 0, :])
                attention(A0, b)
                norm("n1", b, fm[:, 0, 4, :], fm[:, 0, 3, :])
                act.wait_ge(f0["nm"], b + 1)
                for t in range(NT):
                    act.activation(lg[:, t, :], lg[:, t, :], ACT.Exp, bias=gsm[:, t, 0:1],
                                   accum_out=gsm[:, t, 1:2]).then_inc(f0["se"], 1)
                norm("n2", b, fm[:, 1, 1, :], fm[:, 1, 0, :])
                attention(A1, b)
                norm("n4", b, lnw[:, 0, :], None)
                attention(A2, b)
                norm("n5", b, lnw[:, 1, :], None)
                act.wait_ge(m1["df"], b + 1)
                act.activation(gsm[:, :, 1], gsm[:, :, 0], ACT.Exp).then_inc(m1["e1"], 1)
                with act.Fori(0, E // 2) as ep:
                    it = b * (E // 2) + ep
                    for par in range(2):
                        for half in range(2):
                            for f in range(FC):
                                q = (par * 2 + half) * FC + f
                                act.wait_ge(m1["h"], it * 4 * FC + q + 1)
                                act.wait_ge(m1["y"], it * 2 * NT + max((par * 2 + half - 1) * 4, 0))
                                act.activation(H[half][:, f, :], pA[q // 2 % 2][:, q % 2 * 512:q % 2 * 512 + 512],
                                               ACT.Gelu).then_inc(m1["ge"], 1)

        @block.tensor
        def _(pe):
            pe.wait_ge(s_const, N_CONST)
            pe.wait_ge(s_csil, 1)
            for l in range(2):
                if l:
                    pe.wait_ge(s_mrow, 1)
                for c in range(3):
                    for k in range(KC):
                        mm = pe.matmul(pA[c // 2][0:B, c % 2 * 512:c % 2 * 512 + 512], csig[:, l, k, :],
                                       wm_sb[l][:, k, c * 512:c * 512 + 512], start=(k == 0), stop=(k == KC - 1))
                mm.then_inc(s_mmm, 1)
            pe.wait_ge(s_wld, N_WLD)

            def norm(n, b):
                s = ln[n]
                for idx in range(4):
                    half, c = idx // 2, idx % 2
                    if c == 0:
                        pe.wait_ge(s["xn"], b * NT + 4 * half + 4)
                    if idx >= 2:
                        pe.wait_ge(s["ev"], b * 4 + idx - 1)
                    for t in range(4):
                        mm = pe.transpose(pT[idx % 2][:, t * P:t * P + P],
                                          xn[:, 4 * half + t, c * P:c * P + P], ident[:, :])
                    mm.then_inc(s["tr"], 1)

            def project_narrow(a, b, n):
                s = at[a.name]
                pe.wait_ge(ln[n]["ev"], b * 4 + 4)
                pe.wait_ge(s["wn"], b * 16 + 16)
                for c in range(KC):
                    for x in range(2):
                        if c:
                            pe.wait_ge(s["fn"], b * 4 + x + 1)
                        for h in range(2):
                            for k in range(KC):
                                mm = pe.matmul(pA[x][:, h * 512:h * 512 + 512],
                                               wqn[:, k, x * D + c * P:x * D + c * P + P],
                                               hT[:, k, h * 512:h * 512 + 512],
                                               start=(k == 0), stop=(k == KC - 1))
                        mm.then_inc(s["pn"], 1)
                pe.wait_ge(s["fn"], b * 4 + 4)
                for t in range(NT):
                    if t >= 4:
                        pe.wait_ge(s["vn"], b * 4 + t // 2 - 1)
                    for k in range(KC):
                        mm = pe.matmul(pA[t // 2 % 2][:, t % 2 * 512:t % 2 * 512 + 512], hT[:, k, t * P:t * P + P],
                                       wqn[:, k, 2 * D:2 * D + 4 * P], start=(k == 0), stop=(k == KC - 1))
                    mm.then_inc(s["pj"], 1)

            def attention(a, b, n):
                s = at[a.name]
                U, CH = a.units, a.chunk_at[-1]
                nw = 48 if a.bias else 16
                done = s["cp"] if a.topk else s["e"]
                if a.narrow:
                    project_narrow(a, b, n)
                with pe.Fori(0, a.groups) as g:
                    it = b * a.groups + g
                    pe.wait_ge(s["be"], it)
                    pe.wait_ge(done, it * U)
                    if a.narrow:
                        pe.wait_ge(s["vn"], b * 4 + 4)
                        pe.wait_ge(s["st"], (b + 1) * 16 * 2 * KC * len(TERMS))
                    else:
                        pe.wait_ge(ln[n]["ev"], b * 4 + 4)
                        pe.wait_ge(s["w"], it * nw + nw)
                        for w in range(2):
                            for h in range(2):
                                for k in range(KC):
                                    mm = pe.matmul(pA[w][:, h * 512:h * 512 + 512], wq[:, k, w * P:w * P + P],
                                                   hT[:, k, h * 512:h * 512 + 512],
                                                   start=(k == 0), stop=(k == KC - 1))
                            mm.then_inc(s["pj"], 1)
                        pe.wait_ge(s["eqk"], it * (a.hg + 1) + a.hg)
                        for t in range(NT):
                            for k in range(KC):
                                mm = pe.matmul(pA[0][:, t * P:t * P + P], hT[:, k, t * P:t * P + P],
                                               wq[:, k, 2 * P:3 * P], start=(k == 0), stop=(k == KC - 1))
                        mm.then_inc(s["pj"], 1)
                        pe.wait_ge(s["eqk"], it * (a.hg + 1) + a.hg + 1)
                        pe.wait_ge(s["ev"], it + 1)

                    def scores(u):
                        i, j = a.unit(u)
                        if u >= 2:
                            pe.wait_ge(done, it * U + u - 1)
                        w = (i + 1) * P
                        for lo in range(0, w, 512):
                            hi = min(lo + 512, w)
                            if a.narrow:
                                h = g * a.hg + j
                                q = stack[0:KROWS, 0, bass.ds(h, 1), i * P:i * P + P].rearrange("p a n -> p (a n)")
                                k = stack[0:KROWS, 1, bass.ds(h, 1), lo:hi].rearrange("p a n -> p (a n)")
                            else:
                                q, k = qm[:, j, i * P:i * P + P], kT[:, lo:hi]
                            mm = pe.matmul(pA[u % 2][:, lo:hi], q, k, start=True, stop=(hi < w))
                        mm = pe.matmul(pA[u % 2][:, w - P:w], identm[:, :], tri[:, a.mask, :],
                                       start=False, stop=True)
                        mm.then_inc(s["s"], 1)

                    U2 = a.hg * NT // 2

                    def second(u):
                        return max(u - (U - U2), 0)

                    def free(q):
                        if q < 0:
                            pe.wait_ge(s["te"], it * U)
                            pe.wait_ge(s["te2"], it * U2)
                            return
                        u = next(u for u in range(U) if a.chunk_at[u + 1] > q)
                        if q == a.chunk_at[u]:
                            pe.wait_ge(s["te"], it * U + u + 1)
                        else:
                            pe.wait_ge(s["te2"], it * U2 + second(u + 1))

                    def turn(u):
                        i, j = a.unit(u)
                        pe.wait_ge(s["p"] if a.topk else s["e"], it * U + u + 1)
                        for c in range(a.chunks[u]):
                            q = a.chunk_at[u] + c
                            free(q - 2)
                            for kb in range(4 * c, min(4 * c + 4, i + 1)):
                                mm = pe.transpose(pT[q % 2][:, kb % 4 * P:kb % 4 * P + P],
                                                  pr[:, u % 4, kb * P:kb * P + P], ident[:, :])
                            mm.then_inc(s["t"], 1)

                    def values(p):
                        i, j = a.unit(2 * p)
                        pe.wait_ge(s["te"], it * U + 2 * p + 2)
                        if second(2 * p + 2):
                            pe.wait_ge(s["te2"], it * U2 + second(2 * p + 2))
                        if p == 0:
                            pe.wait_ge(s["o"], it)
                            if a.narrow:
                                pe.wait_ge(s["vg"], it + 1)
                        for kb in range(i + 1):
                            for u in (2 * p, 2 * p + 1):
                                j = a.unit(u)[1]
                                sl = slice(j * a.slot, (j + 1) * a.slot)
                                mm = pe.matmul(pO[sl, i * P:i * P + P], vs[:, kb, sl],
                                               prT[:, u % 4, kb * P:kb * P + P],
                                               start=(kb == 0), stop=(kb == i))
                        mm.then_inc(s["pv"], 1)

                    for u in range(2):
                        scores(u)
                    for p in range(a.pairs):
                        for u in (2 * p, 2 * p + 1):
                            if a.topk:
                                if u + 2 < U:
                                    scores(u + 2)
                            else:
                                turn(u)
                                if u + 2 < U:
                                    scores(u + 2)
                        if a.topk:
                            if p >= 1:
                                turn(2 * p - 2)
                                turn(2 * p - 1)
                            if p >= 2:
                                values(p - 2)
                        elif p >= 1:
                            values(p - 1)
                    if a.topk:
                        turn(U - 2)
                        turn(U - 1)
                        values(a.pairs - 2)
                    values(a.pairs - 1)
                    pe.wait_ge(s["ri"], it + 1)
                    pe.wait_ge(done, it * U + U)
                    for i in range(NT):
                        for j in range(a.hg):
                            sl = slice(j * a.slot, (j + 1) * a.slot)
                            u = i * a.hg + j
                            mm = pe.matmul(pA[0][sl, i * P:i * P + P],
                                           rinv[:, u:u + 1].to_broadcast([P, a.slot]), ident[:, :],
                                           start=True, stop=True)
                    mm.then_inc(s["bc"], 1)
                pe.wait_ge(s["o"], b * a.groups + a.groups)
                pe.wait_ge(s["wo"], b * 16 + 16)
                pe.wait_ge(s["te"], (b * a.groups + a.groups) * U)
                pe.wait_ge(s["te2"], (b * a.groups + a.groups) * (U // 2))
                oall = oall_n if a.narrow else oall_w
                for t in range(NT):
                    if t >= 2:
                        pe.wait_ge(s["x"], b * NT + t - 1)
                    for g in range(a.groups):
                        mm = pe.matmul(pT[t % 2][:, 0:D], oall[:, g, t * P:t * P + P], wo_sb[:, g, :],
                                       start=(g == 0), stop=(g == a.groups - 1))
                    mm.then_inc(s["y"], 1)

            with pe.Fori(0, B) as b:
                pe.wait_ge(s_bld, b * 128 + 128)
                pe.transpose(pT[0][:, 0:P], fmr[:, :], ident[:, :]).then_inc(s_fmt, 1)
                pe.wait_ge(s_fm, b + 1)
                norm("n0", b)
                attention(A0, b, "n0")
                norm("n1", b)
                pe.wait_ge(ln["n1"]["ev"], b * 4 + 4)
                for t in range(NT):
                    if t >= 2:
                        pe.wait_ge(f0["le"], b * NT + t - 1)
                    for k in range(KC):
                        mm = pe.matmul(pT[t % 2][:, 0:D], hT[:, k, t * P:t * P + P], wg[:, k, :],
                                       start=(k == 0), stop=(k == KC - 1))
                    mm.then_inc(f0["lg"], 1)
                pe.wait_ge(f0["g"], b + 1)
                for t in range(NT):
                    mm = pe.transpose(pT[t // 4][0:E, t % 4 * P:t % 4 * P + P], gate[:, t, :], ident[:, :])
                mm.then_inc(f0["gt"], 1)
                pe.wait_ge(f0["ge"], b * 2 + 2)
                pe.wait_ge(f0["w"], b * 16 + 16)
                for t in range(NT):
                    if t >= 2:
                        pe.wait_ge(f0["x"], b * NT + t - 1)
                    pe.matmul(pT[t % 2][:, 0:D], gT[:, t * P:t * P + P], be[:, :], start=True, stop=True)\
                      .then_inc(f0["yb"], 1)
                    for half in range(2):
                        if t >= 1:
                            pe.wait_ge(f0["yc"], b * 2 * NT + 2 * t + half - 1)
                        for e2 in range(2):
                            e = 4 * half + 2 * e2
                            for k in range(KC):
                                mm = pe.matmul(pA[half][:, e2 * 512:e2 * 512 + 512], hT[:, k, t * P:t * P + P],
                                               we[:, k, e:e + 2, :], start=(k == 0), stop=(k == KC - 1))
                        mm.then_inc(f0["y"], 1)
                norm("n2", b)
                attention(A1, b, "n2")
                norm("n4", b)
                attention(A2, b, "n4")
                norm("n5", b)
                pe.wait_ge(ln["n5"]["ev"], b * 4 + 4)
                for t in range(NT):
                    for k in range(KC):
                        mm = pe.matmul(pT[0][:, t * E:t * E + E], hT[:, k, t * P:t * P + P], rw[:, k, :],
                                       start=(k == 0), stop=(k == KC - 1))
                mm.then_inc(m1["lg"], 1)
                with pe.Fori(0, E // 2) as ep:
                    pe.wait_ge(m1["g"], b + 1)
                    it = b * (E // 2) + ep

                    def hidden(r):
                        par, half = r // 2, r % 2
                        if half == 0:
                            pe.wait_ge(m1["w%d" % par], it * 32 + 32)
                        for f in range(FC):
                            q = r * FC + f
                            pe.wait_ge(m1["ge"], it * 4 * FC + max(q - 3, 0))
                            for k in range(KC):
                                mm = pe.matmul(pA[q // 2 % 2][:, q % 2 * 512:q % 2 * 512 + 512],
                                               w1_sb[par][:, k, f * P:f * P + P],
                                               hT[:, k, half * 512:half * 512 + 512],
                                               start=(k == 0), stop=(k == KC - 1))
                            mm.then_inc(m1["h"], 1)

                    def down(r):
                        par, half = r // 2, r % 2
                        pe.wait_ge(m1["ge"], it * 4 * FC + (r + 1) * FC)
                        for t in range(4):
                            q = r * 4 + t
                            pe.wait_ge(m1["z"], it * 2 * NT + max(q - 1, 0))
                            for f in range(FC):
                                mm = pe.matmul(pT[q % 2][:, 0:D], H[half][:, f, t * P:t * P + P],
                                               w2_sb[par][:, f, :], start=(f == 0), stop=(f == FC - 1))
                            mm.then_inc(m1["y"], 1)

                    hidden(0)
                    for r in range(1, 4):
                        hidden(r)
                        down(r - 1)
                    down(3)

        @block.vector
        def _(v):
            ch = Chain(v, dv)
            v.wait_ge(s_cexp, 1)
            n = ch.mark(v.tensor_scalar(csig[:, :, :, :], csig[:, :, :, :], 1.0, None, ALU.add))
            ch.need(n)
            n = ch.mark(v.reciprocal(csig[:, :, :, :], csig[:, :, :, :]))
            ch.need(n)
            v.tensor_tensor(csig[:, :, :, :], csig[:, :, :, :], ctile[:, :, :, :], ALU.mult).then_inc(s_csil, 1)
            for l in range(2):
                v.wait_ge(s_mmm, l + 1)
                if l:
                    v.wait_ge(s_mst, 16)
                ch.mark(v.tensor_copy(modrow[:, 0:N], pA[0][0:B, :]))
                n = ch.mark(v.tensor_copy(modrow[:, N:6 * D], pA[1][0:B, 0:512]))
                ch.need(n)
                for j in (1, 4):
                    ch.mark(v.tensor_scalar(modrow[:, j * D:j * D + D], modrow[:, j * D:j * D + D], 1.0, None,
                                            ALU.add))
                for j in (2, 5):
                    r = modrow[:, j * D:j * D + D]
                    ch.mark(v.scalar_tensor_tensor(out=modtmp, in0=r, scalar=-1.0, in1=r, op0=ALU.mult,
                                                   op1=ALU.max))
                    n = ch.mark(v.tensor_scalar(modsgn, r, 0.0, 2.0, ALU.is_ge, ALU.mult))
                    ch.need(n)
                    n = ch.mark(v.tensor_scalar(modtmp, modtmp, 0.25, None, ALU.max))
                    ch.need(n)
                    n = ch.mark(v.scalar_tensor_tensor(out=r, in0=modsgn, scalar=-1.0, in1=modtmp, op0=ALU.add,
                                                       op1=ALU.mult))
                    ch.need(n)
                v.sem_inc(s_mrow, 1)
            ch.restart()
            v.wait_ge(s_wld, N_WLD)
            v.wait_ge(s_const, N_CONST)

            def norm(n, b, src):
                s = ln[n]
                at0 = ch.n
                for t in range(NT):
                    ch.mark(v.bn_stats(st[:, t, :], src[:, t, :]))
                for t in range(NT):
                    ch.need(at0 + t + 1)
                    k = ch.mark(v.bn_aggr(mv[:, t, :], st[:, t, :]))
                ch.need(k)
                v.tensor_scalar(ve[:, :], mv[:, :, 1], EPS, None, ALU.add).then_inc(s["var"], 1)
                for t in range(NT):
                    if t == 0:
                        v.wait_ge(s["rs"], b + 1)
                    v.tensor_scalar(xn[:, t, :], src[:, t, :], mv[:, t, 0:1], rstd[:, t:t + 1],
                                    ALU.subtract, ALU.mult).then_inc(s["xn"], 1)

            def attention(a, b):
                s = at[a.name]
                U, CH = a.units, a.chunk_at[-1]
                nw = 48 if a.bias else 16
                if a.narrow:
                    for c in range(KC):
                        for x in range(2):
                            q = 2 * c + x
                            v.wait_ge(s["hn"], b * 8 + 4 * c + x + 1)
                            v.tensor_tensor(full[:, q, :], full[:, q, :], part[:, 4 * c + 2 * x, :], ALU.subtract)\
                             .then_inc(s["rn"], 1)
                        for x in range(2):
                            q = 2 * c + x
                            v.wait_ge(s["hn"], b * 8 + 4 * c + x + 3)
                            v.tensor_tensor(lowp[:, q, :], full[:, q, :], part[:, 4 * c + 2 * x + 1, :],
                                            ALU.subtract).then_inc(s["rn"], 1)
                    for t2 in range(4):
                        v.wait_ge(s["pj"], b * NT + 2 * t2 + 2)
                        psv = pA[t2 % 2][:, :].rearrange("p (t g d) -> p g t d", t=2, d=P)
                        if a.bias:
                            v.tensor_tensor(vall[:, :, 2 * t2:2 * t2 + 2, :], psv,
                                            bv_n[:, :].rearrange("p (g d) -> p g d", d=P).unsqueeze(2)
                                            .to_broadcast([P, 4, 2, P]), ALU.add)\
                             .then_inc(s["vn"], 1)
                        else:
                            v.tensor_copy(vall[:, :, 2 * t2:2 * t2 + 2, :], psv).then_inc(s["vn"], 1)
                ch.restart()
                with v.Fori(0, a.groups) as g:
                    it = b * a.groups + g
                    if not a.narrow:
                        v.wait_ge(s["w"], it * nw + nw)
                        v.wait_ge(s["pj"], it * 3 + 3)
                        psv = pA[0][:, :].rearrange("p (t n) -> p t n", n=P)
                        v.tensor_tensor(vs[:, :, :], psv, bv_bc[:, :].unsqueeze(1).to_broadcast([P, NT, P]),
                                        ALU.add).then_inc(s["ev"], 1)

                    def select(p):
                        us = (2 * p, 2 * p + 1)
                        i = a.unit(us[0])[0]
                        w = (i + 1) * P
                        last = {}
                        if p:
                            ch.need(ch.n)
                        v.wait_ge(s["k"], it * U + max(us[0] - 2, 0))
                        v.wait_ge(s["cp"], it * U + us[0] + 2)
                        ch.mark(v.memset(step[:, :], 0.0))
                        for u in us:
                            last[u] = ch.mark(v.max(vals[:, u % 4, 0:8], ssb[:, u % 4, 0:w]))
                        ch.need(last[us[1]])
                        v.wait_ge(s["e"], it * U + max(us[0] - 2, 0))
                        c = us[0] % 4
                        v.tensor_scalar(nmax[:, c:c + 2], vals[:, c:c + 2, 0], -1.0, None, ALU.mult)\
                         .then_inc(s["mx"], 1)
                        for r in range(TOPK // 8 - 1):
                            for u in us:
                                ch.need(last[u])
                                src = ssb[:, u % 4, 0:w] if r == 0 else work[:, u % 2, 0:w]
                                last[u] = ch.mark(v.match_replace(
                                    out=work[:, u % 2, 0:w], in_to_replace=vals[:, u % 4, 8 * r:8 * r + 8],
                                    in_values=src, imm_value=NEG_REPLACED))
                            for u in us:
                                ch.need(last[u])
                                m = v.max(vals[:, u % 4, 8 * r + 8:8 * r + 16], work[:, u % 2, 0:w])
                                if r < TOPK // 8 - 2:
                                    last[u] = ch.mark(m)
                                else:
                                    m.then_inc(s["th"], 1)

                    def rowmax(u):
                        w = (a.unit(u)[0] + 1) * P
                        v.wait_ge(s["s"], it * U + u + 1)
                        v.wait_ge(s["e"], it * U + max(u - 3, 0))
                        v.tensor_reduce(nmax[:, u % 4:u % 4 + 1], pA[u % 2][:, 0:w], AX, ALU.max,
                                        negate=True).then_inc(s["mx"], 1)

                    def out_of_psum(u):
                        i, j = a.unit(u)
                        for c in range(1):
                            q = a.chunk_at[u] + c
                            w = min(i + 1 - 4 * c, 4) * P
                            v.wait_ge(s["t"], it * CH + q + 1)
                            v.wait_ge(s["pv"], it * a.pairs + max(u // 2 - 1, 0))
                            v.tensor_copy(prT[:, u % 4, c * 512:c * 512 + w], pT[q % 2][:, 0:w])\
                             .then_inc(s["te"], 1)

                    if a.topk:
                        for p in range(a.pairs):
                            select(p)
                        v.wait_ge(s["rs"], it * U + U)
                    else:
                        rowmax(0)
                        for u in range(U):
                            if u + 1 < U:
                                rowmax(u + 1)
                            out_of_psum(u)
                        v.wait_ge(s["e"], it * U + U)
                    v.reciprocal(rinv[:, 0:U], rsum[:, 0:U]).then_inc(s["ri"], 1)
                    v.wait_ge(s["pv"], it * a.pairs + a.pairs)
                    v.wait_ge(s["be"], it + 1)
                    v.tensor_tensor((oall_n if a.narrow else oall_w)[:, bass.ds(g, 1), :].rearrange("p a n -> p (a n)"), pO[:, :], rbc,
                                    ALU.mult).then_inc(s["o"], 1)
                    ch.restart()

            def project(a, b, dst, bias, gate_row):
                s = at[a.name]
                for t in range(NT):
                    v.wait_ge(s["y"], b * NT + t + 1)
                    y = pT[t % 2][:, 0:D]
                    if bias is not None:
                        n = ch.mark(v.tensor_tensor(tmp[t % 2][:, :], y, bias, ALU.add))
                        ch.need(n)
                        n = ch.mark(v.tensor_tensor(tmp[t % 2][:, :], tmp[t % 2][:, :], gate_row, ALU.mult))
                        ch.need(n)
                        y = tmp[t % 2][:, :]
                    v.tensor_tensor(dst[:, t, :], dst[:, t, :], y, ALU.add).then_inc(s["x"], 1)
                v.wait_ge(s["x"], b * NT + NT)

            with v.Fori(0, B) as b:
                v.wait_ge(s_bld, b * 128 + 128)
                norm("n0", b, X)
                attention(A0, b)
                project(A0, b, X, bo_bc[:, 0, :], bc[:, 0, :])
                norm("n1", b, X)
                for t in range(NT):
                    v.wait_ge(f0["lg"], b * NT + t + 1)
                    v.tensor_tensor(lg[:, t, :], pT[t % 2][:, 0:D], bg_bc[:, :], ALU.add).then_inc(f0["le"], 1)
                second = ch.n
                v.wait_ge(f0["le"], b * NT + NT)
                v.memset(ixf[:, :, :], 0.0)
                for t in range(NT):
                    ch.mark(v.max(v8[:, t, :], lg[:, t, :]))
                for t in range(NT):
                    ch.need(second + t + 1)
                    ch.mark(v.max_index(ix8[:, t, :], v8[:, t, :], lg[:, t, :]))
                ch.need(ch.n)
                v.tensor_scalar(gsm[:, :, 0], v8[:, :, 0], -1.0, None, ALU.mult).then_inc(f0["nm"], 1)
                n = ch.mark(v.tensor_scalar(ix8[:, :, 1], ix8[:, :, 0], E - 1, None, ALU.bitwise_and))
                ch.need(n)
                n = ch.mark(v.tensor_copy(ixf[:, :, 0], ix8[:, :, 1]))
                ch.need(n)
                iota_bc = iota8[:, :].unsqueeze(1).to_broadcast([P, NT, E])
                n = ch.mark(v.tensor_tensor(gate[:, :, :], iota_bc, ixf[:, :, 0:1].to_broadcast([P, NT, E]),
                                            ALU.is_equal))
                v.wait_ge(f0["se"], b * NT + NT)
                n = ch.mark(v.reciprocal(gsm[:, :, 2], gsm[:, :, 1]))
                ch.need(n)
                m = v.tensor_tensor(gate[:, :, :], gate[:, :, :], gsm[:, :, 2:3].to_broadcast([P, NT, E]), ALU.mult)
                m.then_inc(f0["g"], 1)
                v.wait_ge(f0["gt"], b + 1)
                for h in range(2):
                    v.tensor_copy(gT[:, h * 512:h * 512 + 512], pT[h][0:E, :]).then_inc(f0["ge"], 1)
                for t in range(NT):
                    made = [0, 0]
                    for e in range(E):
                        c = e % 2
                        src = pA[e // 4][:, e % 4 * D:e % 4 * D + D]
                        if e % 4 == 0:
                            v.wait_ge(f0["y"], b * 2 * NT + 2 * t + e // 4 + 1)
                        if e < 2:
                            m = v.tensor_scalar(acc[c], src, gate[:, t, e:e + 1], None, ALU.mult)
                        else:
                            if made[c] is None:
                                v.wait_ge(f0["yc"], b * 2 * NT + 2 * t + 1)
                            else:
                                ch.need(made[c])
                            m = v.scalar_tensor_tensor(out=acc[c], in0=src, scalar=gate[:, t, e:e + 1],
                                                       in1=acc[c], op0=ALU.mult, op1=ALU.add)
                        if e % 4 == 3:
                            m.then_inc(f0["yc"], 1)
                            made[c] = None
                        else:
                            made[c] = ch.mark(m)
                    ch.need(made[0])
                    v.wait_ge(f0["yc"], b * 2 * NT + 2 * t + 2)
                    n = ch.mark(v.tensor_tensor(acc[2], acc[0], acc[1], ALU.add))
                    v.wait_ge(f0["yb"], b * NT + t + 1)
                    ch.need(n)
                    n = ch.mark(v.tensor_tensor(acc[3], acc[2], pT[t % 2][:, 0:D], ALU.add))
                    ch.need(n)
                    n = ch.mark(v.scalar_tensor_tensor(out=tmp[0][:, :], in0=acc[3], scalar=0.0, in1=bc[:, 1, :],
                                                       op0=ALU.max, op1=ALU.mult))
                    ch.need(n)
                    m = v.tensor_tensor(X[:, t, :], X[:, t, :], tmp[0][:, :], ALU.add)
                    m.then_inc(f0["x"], 1)
                v.wait_ge(f0["x"], b * NT + NT)
                norm("n2", b, X)
                attention(A1, b)
                project(A1, b, X, bo_bc[:, 1, :], bc[:, 2, :])
                norm("n3", b, X)
                v.wait_ge(ln["n3"]["xn"], b * NT + NT)
                for t in range(NT):
                    n = ch.mark(v.tensor_tensor(Z[:, t, :], xn[:, t, :], bc[:, 4, :], ALU.mult))
                ch.need(n)
                for t in range(NT):
                    n = ch.mark(v.tensor_tensor(Z[:, t, :], Z[:, t, :], bc[:, 3, :], ALU.add))
                ch.need(n)
                norm("n4", b, Z)
                attention(A2, b)
                project(A2, b, Z, None, None)
                norm("n5", b, Z)
                v.wait_ge(m1["lg"], b + 1)
                n = ch.mark(v.tensor_copy(gate2[:, :, :], pT[0][:, 0:NT * E].rearrange("p (t e) -> p t e", e=E)))
                ch.need(n)
                for t in range(NT):
                    n = ch.mark(v.max(v8[:, t, :], gate2[:, t, :]))
                ch.need(n)
                v.tensor_tensor(gsm[:, :, 0], v8[:, :, 1], v8[:, :, 0], ALU.subtract).then_inc(m1["df"], 1)
                for t in range(NT):
                    n = ch.mark(v.max_index(ix8[:, t, :], v8[:, t, :], gate2[:, t, :]))
                ch.need(n)
                n = ch.mark(v.tensor_copy(ixf[:, :, :], ix8[:, :, 0:2]))
                v.wait_ge(m1["e1"], b + 1)
                n = ch.mark(v.tensor_scalar(gsm[:, :, 2], gsm[:, :, 1], 1.0, None, ALU.add))
                ch.need(n)
                n = ch.mark(v.reciprocal(gsm[:, :, 3], gsm[:, :, 2]))
                ch.need(n)
                n = ch.mark(v.tensor_tensor(gsm[:, :, 4], gsm[:, :, 1], gsm[:, :, 3], ALU.mult))
                for r, dst in ((0, gate), (1, gate2)):
                    n = ch.mark(v.tensor_tensor(dst[:, :, :], iota_bc, ixf[:, :, r:r + 1].to_broadcast([P, NT, E]),
                                                ALU.is_equal))
                ch.need(n)
                for r, dst in ((0, gate), (1, gate2)):
                    n = ch.mark(v.tensor_tensor(dst[:, :, :], dst[:, :, :],
                                                gsm[:, :, 3 + r:4 + r].to_broadcast([P, NT, E]), ALU.mult))
                ch.need(n)
                m = v.tensor_tensor(gate[:, :, :], gate[:, :, :], gate2[:, :, :], ALU.add)
                m.then_inc(m1["g"], 1)
                ch.restart()
                with v.Fori(0, E // 2) as ep:
                    it = b * (E // 2) + ep
                    for q in range(2 * NT):
                        par, t = q // NT, q % NT
                        v.wait_ge(m1["y"], it * 2 * NT + q + 1)
                        v.wait_ge(m1["z"], it * 2 * NT + max(q - NT + 1, 0))
                        v.scalar_tensor_tensor(out=Z[:, t, :], in0=pT[q % 2][:, 0:D],
                                               scalar=gate[:, t, bass.ds(ep * 2 + par, 1)], in1=Z[:, t, :],
                                               op0=ALU.mult, op1=ALU.add).then_inc(m1["z"], 1)
                v.wait_ge(m1["z"], b * E * NT + E * NT)
                for t in range(NT):
                    n = ch.mark(v.tensor_tensor(Z[:, t, :], Z[:, t, :], bc[:, 5, :], ALU.mult))
                ch.need(n)
                for t in range(NT):
                    n = ch.mark(v.tensor_tensor(X[:, t, :], X[:, t, :], Z[:, t, :], ALU.add))
                ch.need(n)
                v.sem_inc(s_fin, 1)
                ch.restart()


_INS = ["x", "ct", "wmod0", "wmod1", "wqkv0", "wqkv1", "wqkv2", "bqk0", "bqk1", "bv0", "bv1", "wo0", "wo1", "wo2",
        "bo0", "bo1", "ffn_wg", "ffn_bg", "ffn_we", "ffn_be", "ln_w", "router_w", "w1", "w2"]


def kernel(**inp):
    import numpy as np
    import concourse.bacc as _bacc
    from concourse.bass_utils import run_bass_kernel_spmd as _run

    def slots(w, slot):
        w = np.asarray(w)
        d = w.shape[-1] // 16
        w = w.reshape(w.shape[:-1] + (16, d))
        if d < slot:
            pad = np.zeros(w.shape[:-1] + (slot - d,), w.dtype)
            w = np.concatenate([w, pad], axis=-1)
        return w.reshape(w.shape[:-2] + (16 * slot // P, P))

    def group(wq, wk, wv, slot):
        ws = [slots(w, slot).reshape(KC, P, -1, P).transpose(2, 1, 0, 3) for w in (wq, wk, wv)]
        return np.ascontiguousarray(np.concatenate(ws, axis=3))

    def spread(w):
        w = np.asarray(w)
        return w.reshape(w.shape[:-1] + (KC, 8, 16)).swapaxes(-1, -2).reshape(w.shape)

    def narrow(wq, wk, wv):
        wq, wk = spread(wq), spread(wk)
        w = np.concatenate([wq, wk, slots(wv, 32).reshape(D, 4 * P)], axis=1)
        return np.ascontiguousarray(w.reshape(KC, P, N).transpose(1, 0, 2))

    def out_weights(w, slot):
        return np.ascontiguousarray(slots(np.asarray(w).T, slot).transpose(2, 1, 0))

    a = {k: np.asarray(v) for k, v in inp.items()}
    qkv = a["L1_attn_W_qkv"].reshape(D, 3, N)
    bqkv = a["L1_attn_b_qkv"].reshape(3, N)
    cat = a["L1_ffn_c_attn_w"].reshape(D, 3, D)
    arr = {
        "x": a["L0_attn_x"],
        "ct": np.ascontiguousarray(np.stack([a["L0_c"], a["L1_c"]]).reshape(2, B, KC, P).transpose(3, 0, 2, 1)),
        "wmod0": a["L0_wmod"], "wmod1": a["L1_wmod"],
        "wqkv0": narrow(a["L0_attn_Wq"].T, a["L0_attn_Wk"].T, a["L0_attn_Wv"].T),
        "wqkv1": group(qkv[:, 0], qkv[:, 1], qkv[:, 2], 64),
        "wqkv2": narrow(cat[:, 0], cat[:, 1], cat[:, 2]),
        "bqk0": np.ascontiguousarray(spread(np.stack([a["L0_attn_bq"], a["L0_attn_bk"]])).reshape(2, KC, P).transpose(2, 0, 1)),
        "bqk1": np.ascontiguousarray(np.stack([slots(bqkv[0], 64), slots(bqkv[1], 64)], axis=2)),
        "bv0": np.ascontiguousarray(slots(a["L0_attn_bv"], 32).reshape(4 * P)),
        "bv1": np.ascontiguousarray(slots(bqkv[2], 64)),
        "wo0": out_weights(a["L0_attn_Wo"].T, 32),
        "wo1": out_weights(a["L1_attn_W_out"], 64),
        "wo2": out_weights(a["L1_ffn_c_proj_w"], 32),
        "bo0": a["L0_attn_bo"], "bo1": a["L1_attn_b_out"],
        "ffn_wg": a["L0_ffn_Wg"], "ffn_bg": a["L0_ffn_bg"], "ffn_we": np.ascontiguousarray(a["L0_ffn_We"].reshape(E, KC, P, D).transpose(2, 1, 0, 3)),
         "ffn_be": a["L0_ffn_be"],
        "ln_w": np.ascontiguousarray(np.stack([a["L1_ffn_ln1_w"], a["L1_ffn_ln2_w"]]).reshape(2, KC, P)
                                     .transpose(2, 0, 1)),
        "router_w": a["L1_ffn_router_w"],
        "w1": np.ascontiguousarray(a["L1_ffn_w1"].reshape(KC, P, E, F).transpose(2, 1, 0, 3)),
        "w2": np.ascontiguousarray(a["L1_ffn_w2"].reshape(E, FC, P, D).transpose(0, 2, 1, 3)),
    }
    nc = _bacc.Bacc("TRN2", target_bir_lowering=False, num_devices=1)
    ap, arrays = {}, {}
    for name in _INS:
        arrays[f"in_{name}"] = np.ascontiguousarray(arr[name])
        ap[name] = nc.dram_tensor(f"in_{name}", arr[name].shape, F32, kind="ExternalInput").ap()
    out = nc.dram_tensor("out_0", (B, N, D), F32, kind="ExternalOutput").ap()
    build(nc, ap["x"], ap["ct"], [ap["wmod0"], ap["wmod1"]], [ap["wqkv0"], ap["wqkv1"], ap["wqkv2"]],
          [ap["bqk0"], ap["bqk1"]], [ap["bv0"], ap["bv1"]], [ap["wo0"], ap["wo1"], ap["wo2"]],
          [ap["bo0"], ap["bo1"]], ap["ffn_wg"], ap["ffn_bg"], ap["ffn_we"], ap["ffn_be"], ap["ln_w"],
          ap["router_w"], ap["w1"], ap["w2"], out)
    r = _run(nc, [arrays], core_ids=[0])
    return r.results[0]["out_0"]
```

```python
from contextlib import ExitStack

import concourse.bass as bass
from concourse import mybir

F32 = mybir.dt.float32
BF16 = mybir.dt.bfloat16
U32 = mybir.dt.uint32
ALU = mybir.AluOpType
ACT = mybir.ActivationFunctionType
AX = mybir.AxisListType.X

P = 128
B = 4
N = 1024
D = 256
NT = N // P
KC = D // P
EPS = 1e-5
TOPK = 32
E = 8
F = 512
FC = F // P
NEG_REPLACED = -3.0e38


class Attn:

    def __init__(self, name, slot, head, topk, bias, mask):
        self.name, self.slot, self.topk, self.bias = name, slot, topk, bias
        self.hg = P // slot
        self.groups = 16 // self.hg
        self.scale = float(head) ** -0.5
        self.mask = mask
        self.narrow = head == 16
        self.units = NT * self.hg
        self.pairs = self.units // 2
        self.even = 0 if self.narrow else 1
        self.order = (0, 2, 4, 6, 7, 5, 3, 1) if topk or slot == 64 else tuple(range(NT))
        self.chunks = [(i // 4 + 1) for i in self.order for _ in range(self.hg)]
        self.chunk_at = [sum(self.chunks[:u]) for u in range(self.units + 1)]

    def unit(self, u):
        return self.order[u // self.hg], u % self.hg

    def unit_of(self, i, j):
        return self.order.index(i) * self.hg + j

    def seconds(self, u):
        return sum(c == 2 for c in self.chunks[:u])

    def units_before(self, u, back, first):
        n = u - back + 1
        return max(n, 0) if first else n

    def chunks_before(self, u, back, first):
        n = self.units_before(u, back, first)
        return self.chunk_at[n] if n >= 0 else self.chunk_at[n + self.units] - self.chunk_at[-1]

    def each_group(self, eng, b, group, tail):
        with eng.Fori(0, 1) as g:
            group(g, b * self.groups + g, True)
        with eng.Fori(1, self.groups) as g:
            group(g, b * self.groups + g, False)
        tail(self.groups - 1, b * self.groups + (self.groups - 1))


A0 = Attn("a0", 32, 16, True, True, 0)
A1 = Attn("a1", 64, 64, False, True, 1)
A2 = Attn("a2", 32, 16, False, False, 0)
LNS = ["n0", "n1", "n2", "n3", "n4", "n5"]


class Chain:

    def __init__(self, eng, sem):
        self.eng, self.sem, self.n = eng, sem, 0

    def mark(self, ins):
        ins.then_inc(self.sem, 1)
        self.n += 1
        return self.n

    def need(self, n):
        self.eng.wait_ge(self.sem, n)

    def restart(self):
        self.eng.wait_ge(self.sem, self.n)
        self.eng.sem_clear(self.sem)
        self.n = 0


def build(nc, x, ct, wmod, wqkv, bqk, bv, wo, bo, ffn_wg, ffn_bg, ffn_we, ffn_be, ln_w, router_w, w1, w2, out):
    ctx = ExitStack()
    with ctx:
        def sb(name, shape, dt=F32):
            return ctx.enter_context(nc.sbuf_tensor(name, shape, dt))

        def ps(name, shape, dt=F32):
            return ctx.enter_context(nc.psum_tensor(name, shape, dt))

        def sem(name):
            return ctx.enter_context(nc.semaphore(name))

        mod_dram = nc.dram_tensor("mod_rows", (B, 2, 6, D), F32, kind="Internal").ap()

        pA = [ps(f"pA{i}", [P, N]) for i in range(2)]
        pT = [ps(f"pT{i}", [P, 512]) for i in range(2)]
        pO = ps("pO", [P, N])

        ident = sb("ident", [P, P])
        identm = sb("identm", [P, P], BF16)
        tri = sb("tri", [P, 2, P], BF16)
        iota8 = sb("iota8", [P, E])
        mhalf = sb("mhalf", [P, NT])
        ctile = sb("ctile", [P, 2, KC, B])
        csig = sb("csig", [P, 2, KC, B])
        wg = sb("wg", [P, KC, D])
        bg_bc = sb("bg_bc", [P, D])
        be = sb("be", [E, D])
        lnw = sb("lnw", [P, 2, KC])
        rw = sb("rw", [P, KC, E])
        bo_bc = sb("bo_bc", [P, 2, D])

        X = sb("X", [P, NT, D])
        Z = sb("Z", [P, NT, D])
        hT = sb("hT", [P, KC, N])
        fmr = sb("fmr", [P, P])
        fm = sb("fm", [P, 2, 6, KC])
        bc = sb("bc", [P, 6, D])
        st = sb("st", [P, NT, 6])
        mv = sb("mv", [P, NT, 2])
        ve = sb("ve", [P, NT])
        rstd = sb("rstd", [P, NT])

        bqk_sb = sb("bqk_sb", [P, 2])
        bq_s = sb("bq_s", [P, 1])
        bv_bc = sb("bv_bc", [P, P])
        stack = sb("stack", [P, 2, 16, N], BF16)
        bqk_n = sb("bqk_n", [P, 2, KC])
        bq_n = sb("bq_n", [P, KC])
        wo_sb = sb("wo_sb", [P, 8, D])
        bv_n = sb("bv_n", [P, 4 * P])
        vs = sb("vs", [P, NT, P])
        oall_n = sb("oall_n", [P, 4, N])
        vall = oall_n[:, :, :].rearrange("p g (t d) -> p g t d", d=P)
        first_half = stack[:, 0, :, :].rearrange("p h n -> p (h n)").bitcast(F32)
        we = first_half[:, 0:4096].rearrange("p (k e n) -> p k e n", k=KC, e=E)
        qm = first_half[:, 4096:4096 + 2 * N].rearrange("p (j n) -> p j n", j=2)
        kT = first_half[:, 6144:6144 + N]
        wq = first_half[:, 7168:7168 + KC * 3 * P].rearrange("p (k n) -> p k n", k=KC)
        oall_w = stack[:, 1, :, :].rearrange("p h n -> p (h n)").bitcast(F32).rearrange("p (g n) -> p g n", g=8)
        ssb = sb("ssb", [P, 4, N])
        work = sb("work", [P, 2, N])
        pr = sb("pr", [P, 4, N])
        prT = sb("prT", [P, 4, N])
        keep = sb("keep", [P, 2, N], BF16)
        junk = sb("junk", [P, 2, N], BF16)
        pool_step = sb("pool_step", [P, 2])
        ones2 = sb("ones2", [P, 2])
        step = sb("step", [P, 2])
        vals = sb("vals", [P, 4, TOPK])
        nmax = sb("nmax", [P, 4])
        rsum = sb("rsum", [P, 32])
        rinv = sb("rinv", [P, 32])
        xn = work[:, :, :].rearrange("p a (t d) -> p (a t) d", d=D)
        rbc = sb("rbc", [P, N])
        wqn = prT[:, :, :].rearrange("p a n -> p (a n)")[:, 0:KC * N].rearrange("p (k n) -> p k n", k=KC)
        full = ssb
        part = pr[:, :, :].rearrange("p a n -> p (a n)").bitcast(BF16).rearrange("p (x n) -> p x n", n=N)
        lowp = work[:, :, :].rearrange("p a n -> p (a n)").bitcast(BF16).rearrange("p (x n) -> p x n", n=N)

        lg = ssb[:, 0:2, :].rearrange("p a (t d) -> p (a t) d", d=D)
        v8 = sb("v8", [P, NT, 8])
        ix8 = sb("ix8", [P, NT, 8], U32)
        ixf = sb("ixf", [P, NT, 2])
        gsm = sb("gsm", [P, NT, 8])
        gate = sb("gate", [P, NT, E])
        gate2 = sb("gate2", [P, NT, E])
        gT = vs[0:E, :, :].rearrange("p t d -> p (t d)")
        acc = [work[:, 1, i * D:(i + 1) * D] for i in range(4)]
        tmp = [rbc[:, i * D:(i + 1) * D] for i in range(2)]
        H = [pr[:, 2 * i:2 * i + 2, :].rearrange("p a (f n) -> p (a f) n", n=512) for i in range(2)]
        w1_sb = [ssb[:, i, :].rearrange("p (k f) -> p k f", k=KC) for i in range(2)]
        w2_sb = [ssb[:, 2 + i, :].rearrange("p (k f) -> p k f", k=FC) for i in range(2)]
        wm_sb = [oall_w[:, 3 * i:3 * i + 3, :].rearrange("p a n -> p (a n)").rearrange("p (k n) -> p k n", k=KC)
                 for i in range(2)]
        modrow = oall_w[0:B, 6:8, :].rearrange("p a n -> p (a n)")[:, 0:6 * D]
        modtmp = ssb[0:B, 0, 0:D]
        modsgn = ssb[0:B, 1, 0:D]

        s_const = sem("s_const")
        s_wld = sem("s_wld")
        s_mld = sem("s_mld")
        s_cexp = sem("s_cexp")
        s_csil = sem("s_csil")
        s_mmm = sem("s_mmm")
        s_mrow = sem("s_mrow")
        s_mst = sem("s_mst")
        s_bld = sem("s_bld")
        s_fmt = sem("s_fmt")
        s_fm = sem("s_fm")
        s_fin = sem("s_fin")
        s_out = sem("s_out")
        s_qz = sem("s_qz")
        dv = sem("dv")
        ac = sem("ac")
        ln = {}
        for n in LNS:
            ln[n] = {k: sem(f"{n}_{k}") for k in (
                "var",
                "rs",
                "xn",
                "tr",
                "ev",
            )}
        only = {"narrow": ("wn", "pn", "fn", "hn", "rn", "st", "vn", "vw", "vg"), "wide": ("w", "eqk", "ev"),
                "topk": ("cp", "th", "k", "p", "rs"), "plain": (), "bias": ("bs",)}
        at = {}
        for a in (A0, A1, A2):
            without = only["wide" if a.narrow else "narrow"] + (() if a.topk else only["topk"])\
                + (() if a.bias else only["bias"])
            at[a.name] = {k: sem(f"{a.name}_{k}") for k in (
                "w",
                "wo",
                "pj",
                "bs",
                "eqk",
                "ev",
                "s",
                "cp",
                "mx",
                "e",
                "wn",
                "pn",
                "fn",
                "hn",
                "rn",
                "st",
                "vn",
                "vw",
                "vg",
                "th",
                "k",
                "p",
                "rs",
                "t",
                "te",
                "te2",
                "pv",
                "ri",
                "bc",
                "be",
                "o",
                "y",
                "x",
            ) if k not in without}
        f0 = {k: sem(f"f0_{k}") for k in (
            "w",
            "lg",
            "le",
            "nm",
            "se",
            "g",
            "gt",
            "ge",
            "y",
            "yb",
            "yc",
            "x",
        )}
        m1 = {k: sem(f"m1_{k}") for k in (
            "w0",
            "w1",
            "lg",
            "df",
            "e1",
            "h",
            "ge",
            "y",
            "z",
        )}

        N_WLD = 16 * 9
        TERMS = ((0, 0), (0, 1), (1, 0), (0, 2), (2, 0), (1, 1))
        KROWS = 16 * len(TERMS)
        gw_d = {a.name: wqkv[n] for n, a in enumerate((A0, A1, A2))}
        block = ctx.enter_context(nc.Block())

        def sums_psum(a):
            return [pA[0][:, 512:N], pA[1][:, 512:N]] if a.narrow else [pT[0][:, :], pT[1][:, :]]

        @block.sync
        def _(sp):
            sp.dma_start(ctile[:, :, :, :], ct).then_inc(s_mld, 16)
            for l in range(2):
                sp.dma_start(wm_sb[l], wmod[l].rearrange("(k p) n -> p k n", p=P)).then_inc(s_mld, 16)
            for dst, src in (
                (wg[:, :, :], ffn_wg.rearrange("(k p) n -> p k n", p=P)),
                (bg_bc[:, :], ffn_bg.partition_broadcast(P)),
                (be[:, :], ffn_be),
                (bqk_n[:, :, :], bqk[0]),
                (bv_n[:, :], bv[0].partition_broadcast(P)),
                (lnw[:, :, :], ln_w),
                (rw[:, :, :], router_w.rearrange("(k p) n -> p k n", p=P)),
                (bo_bc[:, 0, :], bo[0].partition_broadcast(P)),
                (bo_bc[:, 1, :], bo[1].partition_broadcast(P)),
            ):
                sp.dma_start(dst, src).then_inc(s_wld, 16)
            for l in range(2):
                sp.wait_ge(s_mrow, l + 1)
                sp.dma_start(mod_dram[:, l],
                             modrow.rearrange("b (j d) -> b j d", j=6)).then_inc(s_mst, 16)
            sp.wait_ge(s_mst, 32)

            def group_weights(a, g):
                s = at[a.name]
                sp.dma_start(wq, gw_d[a.name][bass.ds(g, 1)].rearrange("a p k n -> (a p) k n"))\
                  .then_inc(s["w"], 16)
                if a.bias:
                    sp.dma_start(bqk_sb[:, :], bqk[1][bass.ds(g, 1)].rearrange("a p n -> (a p) n"))\
                      .then_inc(s["w"], 16)
                    sp.dma_start(bv_bc[:, :], bv[1][bass.ds(g, 1)].partition_broadcast(P)
                                 .rearrange("p a n -> p (a n)")).then_inc(s["w"], 16)

            with sp.Fori(0, B) as b:
                sp.wait_ge(s_out, b * 16)
                sp.dma_start(X[:, :, :], x[bass.ds(b, 1)].rearrange("a (t p) d -> p (a t) d", p=P))\
                  .then_inc(s_bld, 16)
                sp.dma_start(fmr[0:24, :], mod_dram[bass.ds(b, 1)]
                             .rearrange("a l j (c p) -> (a l j c) p", p=P)).then_inc(s_bld, 16)
                for i, (l, j) in enumerate(((0, 2), (0, 5), (1, 2), (1, 3), (1, 4), (1, 5))):
                    sp.dma_start(bc[:, i, :], mod_dram[bass.ds(b, 1), l, j, :].partition_broadcast(P)
                                 .rearrange("p a n -> p (a n)")).then_inc(s_bld, 16)
                prev = None
                for n, a in enumerate((A0, A1, A2)):
                    if prev is not None:
                        sp.wait_ge(at[prev.name]["y"], b * NT + NT)
                    sp.dma_start(wo_sb[:, 0:a.groups, :], wo[n]).then_inc(at[a.name]["wo"], 16)
                    if a.narrow:
                        s = at[a.name]
                        sp.dma_start(wqn, wqkv[n]).then_inc(s["wn"], 16)
                        for c in range(KC):
                            for part_no in range(3):
                                if part_no < 2:
                                    sp.wait_ge(s["hn"], b * 8 + 4 * c + 2 * part_no + 2)
                                else:
                                    sp.wait_ge(s["rn"], b * 8 + 4 * c + 4)
                                for side in range(2):
                                    q = 2 * c + side
                                    src = lowp[:, q, :] if part_no == 2 else part[:, 2 * q + part_no, :]
                                    for t, term in enumerate(TERMS):
                                        if term[side] == part_no:
                                            sp.dma_start(stack[16 * t:16 * t + 16, side, 8 * c:8 * c + 8, :],
                                                         src).then_inc(s["st"], 16)
                    else:
                        group_weights(a, 0)
                        with sp.Fori(0, a.groups - 1) as g:
                            sp.wait_ge(at[a.name]["s"], (b * a.groups + g) * a.units + 2)
                            group_weights(a, g + 1)
                    if a is A0:
                        sp.wait_ge(at["a0"]["y"], b * NT + NT)
                        sp.dma_start(we, ffn_we).then_inc(f0["w"], 16)
                    prev = a
                sp.wait_ge(at["a2"]["y"], b * NT + NT)

                def expert(par, e):
                    sp.dma_start(w1_sb[par], w1[bass.ds(e, 1)].rearrange("a p k n -> (a p) k n"))\
                      .then_inc(m1["w%d" % par], 16)
                    sp.dma_start(w2_sb[par], w2[bass.ds(e, 1)].rearrange("a p k n -> (a p) k n"))\
                      .then_inc(m1["w%d" % par], 16)

                expert(0, 0)
                with sp.Fori(0, E // 2 - 1) as ep:
                    it = b * (E // 2) + ep
                    sp.wait_ge(m1["y"], it * 2 * NT)
                    expert(1, ep * 2 + 1)
                    sp.wait_ge(m1["y"], it * 2 * NT + NT)
                    expert(0, ep * 2 + 2)
                sp.wait_ge(m1["y"], (b * (E // 2) + E // 2 - 1) * 2 * NT)
                expert(1, E - 1)
                sp.wait_ge(s_fin, b + 1)
                sp.dma_start(out[bass.ds(b, 1)].rearrange("a (t p) d -> p (a t) d", p=P), X[:, :, :])\
                  .then_inc(s_out, 16)
            sp.wait_ge(s_out, B * 16)

        @block.gpsimd
        def _(pool):
            c = Chain(pool, s_const)
            c.mark(pool.memset(ident[:, :], 0.0))
            c.mark(pool.memset(identm[:, :], 0.0))
            c.mark(pool.memset(tri[:, :, :], 0.0))
            c.mark(pool.memset(mhalf[:, :], -0.5))
            c.mark(pool.memset(fmr[:, :], 0.0))
            c.mark(pool.memset(ones2[:, :], 1.0))
            c.mark(pool.iota(iota8[:, :], pattern=[[1, E]], base=0, channel_multiplier=0,
                             allow_small_or_imprecise_dtypes=True))
            c.need(c.n)
            c.mark(pool.affine_select(out=ident[:, :], in_=ident[:, :], compare_op=ALU.not_equal, fill=1.0,
                                      base=0, pattern=[[-1, P]], channel_multiplier=1))
            c.mark(pool.affine_select(out=identm[:, :], in_=identm[:, :], compare_op=ALU.not_equal, fill=80.0,
                                      base=0, pattern=[[-1, P]], channel_multiplier=1))
            for m, value in ((0, -(2.0 ** 90)), (1, -125.0)):
                c.mark(pool.affine_select(out=tri[:, m, :], in_=tri[:, m, :], compare_op=ALU.is_ge, fill=value,
                                          base=0, pattern=[[-1, P]], channel_multiplier=1))

            def norm(n, b):
                for h in range(2):
                    pool.wait_ge(ln[n]["var"], b * 2 + h + 1)
                    pool.tensor_tensor(rstd[:, 4 * h:4 * h + 4], ve[:, 4 * h:4 * h + 4], mhalf[:, 0:4], ALU.pow)\
                        .then_inc(ln[n]["rs"], 1)

            def narrow(a, b):
                s = at[a.name]
                U = a.units
                steps = 1 + (a.pairs if a.topk else 0)

                def group(g, it, first):
                    carried = [0]

                    def carrier():
                        pool.wait_ge(s["vw"], it * steps + carried[0])
                        pool.tensor_tensor(pool_step[:, :], ones2[:, :], ones2[:, :], ALU.mult).then_inc(s["vw"], 1)
                        carried[0] += 1

                    def values():
                        pool.wait_ge(s["vn"], b * 4 + 4)
                        pool.wait_ge(s["pv"], it * a.pairs)
                        carrier()
                        pool.tensor_copy(vs[:, :, :], vall[:, bass.ds(g, 1), :, :].rearrange("p a t d -> p (a t) d"))\
                            .then_inc(s["vg"], 1)

                    def select(p):
                        us = (2 * p, 2 * p + 1)
                        w = (a.unit(us[0])[0] + 1) * P
                        pool.wait_ge(s["th"], it * U + 2 * p + 2)
                        pool.wait_ge(s["p"], it * U + 2 * p)
                        carrier()
                        for u in us:
                            pool.tensor_scalar(keep[:, u % 2, 0:w], ssb[:, u % 4, 0:w],
                                               vals[:, u % 4, TOPK - 1:TOPK], None, ALU.is_ge)\
                                .then_inc(s["k"], 1)
                        for u in us:
                            pool.wait_ge(s["k"], it * U + u + 1)
                            pool.wait_ge(s["e"], it * U + u + 1)
                            pool.tensor_tensor(pr[:, u % 4, 0:w], keep[:, u % 2, 0:w], pr[:, u % 4, 0:w],
                                               ALU.mult).then_inc(s["p"], 1)

                    if not a.topk:
                        values()
                        return
                    for p in range(a.pairs):
                        if p == (0 if first else 2):
                            values()
                        select(p)

                a.each_group(pool, b, group, lambda g, it: None)

            with pool.Fori(0, B) as b:
                norm("n0", b)
                narrow(A0, b)
                norm("n1", b)
                pool.memset(qm, 0.0).then_inc(s_qz, 1)
                for n in LNS[2:5]:
                    norm(n, b)
                narrow(A2, b)
                norm("n5", b)
        N_CONST = 11

        @block.scalar
        def _(act):
            chain = Chain(act, ac)
            act.wait_ge(s_mld, 48)
            act.activation(csig[:, :, :, :], ctile[:, :, :, :], ACT.Exp, scale=-1.0).then_inc(s_cexp, 1)
            act.wait_ge(s_wld, N_WLD)

            def norm(n, b, scale, shift):
                s = ln[n]
                for idx in range(4):
                    half, c = idx // 2, idx % 2
                    act.wait_ge(s["tr"], b * 4 + idx + 1)
                    act.activation(hT[:, c, half * 512:half * 512 + 512], pT[idx % 2][:, :], ACT.Identity,
                                   scale=scale[:, c:c + 1],
                                   bias=shift[:, c:c + 1] if shift is not None else 0.0).then_inc(s["ev"], 1)

            def project_narrow(a, b):
                s = at[a.name]
                if a.bias:
                    act.mul(bq_n[:, :], bqk_n[:, 0, :], a.scale).then_inc(s["bs"], 1)
                    act.wait_ge(s["bs"], b + 1)
                for c in range(KC):
                    for x in range(2):
                        q = 2 * c + x
                        act.wait_ge(s["pn"], b * 4 + q + 1)
                        bias = (bq_n if x == 0 else bqk_n[:, 1, :])[:, c:c + 1] if a.bias else 0.0
                        act.activation(full[:, q, :], pA[x][:, :], ACT.Identity, scale=a.scale if x == 0 else 1.0,
                                       bias=bias).then_inc(s["fn"], 1)
                    for x in range(2):
                        q = 2 * c + x
                        act.wait_ge(s["fn"], b * 4 + q + 1)
                        act.activation(part[:, 4 * c + 2 * x, :], full[:, q, :], ACT.Copy).then_inc(s["hn"], 1)
                    for x in range(2):
                        q = 2 * c + x
                        act.wait_ge(s["rn"], b * 8 + 4 * c + x + 1)
                        act.activation(part[:, 4 * c + 2 * x + 1, :], full[:, q, :], ACT.Copy).then_inc(s["hn"], 1)

            def attention(a, b):
                s = at[a.name]
                U, CH = a.units, a.chunk_at[-1]
                nw = 48 if a.bias else 16
                if a.narrow:
                    project_narrow(a, b)
                def row_sum(u, it, first):
                    w = (a.unit(u)[0] + 1) * P
                    act.wait_ge(s["p"], it * U + u + 1)
                    act.wait_ge(s["rs"], it * U + a.units_before(u, 2, first))
                    act.activation(junk[:, u % 2, 0:w], pr[:, u % 4, 0:w], ACT.Copy,
                                   accum_out=rsum[:, u:u + 1]).then_inc(s["rs"], 1)

                def out_of_psum(u, it, c0, first):
                    i, j = a.unit(u)
                    for c in range(c0, a.chunks[u]):
                        q = a.chunk_at[u] + c
                        w = min(i + 1 - 4 * c, 4) * P
                        act.wait_ge(s["t"], it * CH + q + 1)
                        act.wait_ge(s["pv"], it * a.pairs + (max(u // 2 - 1, 0) if first else u // 2 - 1))
                        act.activation(prT[:, u % 4, c * 512:c * 512 + w], pT[q % 2][:, 0:w], ACT.Copy)\
                           .then_inc(s["te"] if c == 0 else s["te2"], 1)

                def inverse(it):
                    act.wait_ge(s["bc"], it + 1)
                    act.wait_ge(s["o"], it)
                    for h in range(2):
                        act.activation(rbc[:, h * 512:h * 512 + 512], sums_psum(a)[h], ACT.Copy).then_inc(s["be"], 1)

                def group(g, it, first):
                    if not a.narrow:
                        act.wait_ge(s["w"], it * nw + nw)
                        act.mul(bq_s[:, :], bqk_sb[:, 0:1], a.scale).then_inc(s["bs"], 1)
                        act.wait_ge(s["bs"], it + 1)
                        act.wait_ge(s_qz, b + 1)
                        act.wait_ge(s["pj"], it * 3 + 1)
                        for j in range(a.hg):
                            sl = slice(j * a.slot, (j + 1) * a.slot)
                            act.activation(qm[sl, j, :], pA[0][sl, :], ACT.Identity, scale=a.scale,
                                           bias=bq_s[sl, :]).then_inc(s["eqk"], 1)
                        act.wait_ge(s["pj"], it * 3 + 2)
                        act.activation(kT, pA[1][:, :], ACT.Identity, bias=bqk_sb[:, 1:2])\
                           .then_inc(s["eqk"], 1)
                        if not first:
                            inverse(it - 1)

                    def copy(u):
                        w = (a.unit(u)[0] + 1) * P
                        act.wait_ge(s["s"], it * U + u + 1)
                        act.wait_ge(s["p"], it * U + a.units_before(u, 4, first))
                        act.activation(ssb[:, u % 4, 0:w], pA[(u + a.even) % 2][:, 0:w], ACT.Copy)\
                           .then_inc(s["cp"], 1)

                    def exp_topk(u):
                        w = (a.unit(u)[0] + 1) * P
                        act.wait_ge(s["mx"], it * a.pairs + u // 2 + 1)
                        act.wait_ge(s["rs"], it * U + a.units_before(u, 4, first))
                        act.wait_ge(s["t"], it * CH + a.chunks_before(u, 4, first))
                        act.activation(pr[:, u % 4, 0:w], ssb[:, u % 4, 0:w], ACT.Exp,
                                       bias=nmax[:, u % 4:u % 4 + 1]).then_inc(s["e"], 1)

                    def exp_plain(u):
                        w = (a.unit(u)[0] + 1) * P
                        if u == 0:
                            act.wait_ge(s["ri"], it)
                        act.wait_ge(s["s"], it * U + u + 1)
                        act.wait_ge(s["mx"], it * U + u + 1)
                        act.wait_ge(s["t"], it * CH + a.chunks_before(u, 4, first))
                        act.activation(pr[:, u % 4, 0:w], pA[(u + a.even) % 2][:, 0:w], ACT.Exp,
                                       bias=nmax[:, u % 4:u % 4 + 1],
                                       accum_out=rsum[:, u:u + 1]).then_inc(s["e"], 1)

                    if a.topk:
                        copy(0)
                        copy(1)
                        for p in range(a.pairs):
                            for u in (2 * p, 2 * p + 1):
                                exp_topk(u)
                            for u in (2 * p + 2, 2 * p + 3):
                                if u < U:
                                    copy(u)
                            if p == 0 and not first:
                                end(it - 1)
                            if p == 1 and not first:
                                act.wait_ge(s["ri"], it)
                            if p >= 1:
                                for u in (2 * p - 2, 2 * p - 1):
                                    row_sum(u, it, first)
                                if p == 1 and not first:
                                    inverse(it - 1)
                                for u in (2 * p - 2, 2 * p - 1):
                                    out_of_psum(u, it, 0, first)
                    else:
                        for u in range(U):
                            exp_plain(u)
                            if a.narrow and u == 1 and not first:
                                inverse(it - 1)
                            if u >= 1:
                                out_of_psum(u - 1, it, 1, first)
                        out_of_psum(U - 1, it, 1, first)

                def end(it):
                    for u in (U - 2, U - 1):
                        row_sum(u, it, False)
                    for u in (U - 2, U - 1):
                        out_of_psum(u, it, 0, False)

                def tail(g, it):
                    if a.topk:
                        end(it)
                    inverse(it)

                a.each_group(act, b, group, tail)

            with act.Fori(0, B) as b:
                act.wait_ge(s_fmt, b + 1)
                act.activation(fm[:, :, :, :].rearrange("p l j c -> p (l j c)"), pT[0][:, 0:24], ACT.Copy)\
                   .then_inc(s_fm, 1)
                act.wait_ge(s_fm, b + 1)
                norm("n0", b, fm[:, 0, 1, :], fm[:, 0, 0, :])
                attention(A0, b)
                norm("n1", b, fm[:, 0, 4, :], fm[:, 0, 3, :])
                act.wait_ge(f0["nm"], b + 1)
                for t in range(NT):
                    act.activation(lg[:, t, :], lg[:, t, :], ACT.Exp, bias=gsm[:, t, 0:1],
                                   accum_out=gsm[:, t, 1:2]).then_inc(f0["se"], 1)
                norm("n2", b, fm[:, 1, 1, :], fm[:, 1, 0, :])
                attention(A1, b)
                norm("n4", b, lnw[:, 0, :], None)
                attention(A2, b)
                norm("n5", b, lnw[:, 1, :], None)
                act.wait_ge(m1["df"], b + 1)
                act.activation(gsm[:, :, 1], gsm[:, :, 0], ACT.Exp).then_inc(m1["e1"], 1)
                with act.Fori(0, E // 2) as ep:
                    it = b * (E // 2) + ep
                    for par in range(2):
                        for half in range(2):
                            for f in range(FC):
                                q = (par * 2 + half) * FC + f
                                act.wait_ge(m1["h"], it * 4 * FC + q + 1)
                                act.wait_ge(m1["y"], it * 2 * NT + max((par * 2 + half - 1) * 4, 0))
                                act.activation(H[half][:, f, :], pA[q // 2 % 2][:, q % 2 * 512:q % 2 * 512 + 512],
                                               ACT.Gelu).then_inc(m1["ge"], 1)

        @block.tensor
        def _(pe):
            pe.wait_ge(s_const, N_CONST)
            pe.wait_ge(s_csil, 1)
            for l in range(2):
                if l:
                    pe.wait_ge(s_mrow, 1)
                for c in range(3):
                    for k in range(KC):
                        mm = pe.matmul(pA[c // 2][0:B, c % 2 * 512:c % 2 * 512 + 512], csig[:, l, k, :],
                                       wm_sb[l][:, k, c * 512:c * 512 + 512], start=(k == 0), stop=(k == KC - 1))
                mm.then_inc(s_mmm, 1)
            pe.wait_ge(s_wld, N_WLD)

            def norm(n, b):
                s = ln[n]
                for idx in range(4):
                    half, c = idx // 2, idx % 2
                    if c == 0:
                        pe.wait_ge(s["xn"], b * NT + 4 * half + 4)
                    if idx >= 2:
                        pe.wait_ge(s["ev"], b * 4 + idx - 1)
                    for t in range(4):
                        mm = pe.transpose(pT[idx % 2][:, t * P:t * P + P],
                                          xn[:, 4 * half + t, c * P:c * P + P], ident[:, :])
                    mm.then_inc(s["tr"], 1)

            def project_narrow(a, b, n):
                s = at[a.name]
                pe.wait_ge(ln[n]["ev"], b * 4 + 4)
                pe.wait_ge(s["wn"], b * 16 + 16)
                for c in range(KC):
                    for x in range(2):
                        if c:
                            pe.wait_ge(s["fn"], b * 4 + x + 1)
                        for h in range(2):
                            for k in range(KC):
                                mm = pe.matmul(pA[x][:, h * 512:h * 512 + 512],
                                               wqn[:, k, x * D + c * P:x * D + c * P + P],
                                               hT[:, k, h * 512:h * 512 + 512],
                                               start=(k == 0), stop=(k == KC - 1))
                        mm.then_inc(s["pn"], 1)
                pe.wait_ge(s["fn"], b * 4 + 4)
                for t in range(NT):
                    if t >= 4:
                        pe.wait_ge(s["vn"], b * 4 + t // 2 - 1)
                    for k in range(KC):
                        mm = pe.matmul(pA[t // 2 % 2][:, t % 2 * 512:t % 2 * 512 + 512], hT[:, k, t * P:t * P + P],
                                       wqn[:, k, 2 * D:2 * D + 4 * P], start=(k == 0), stop=(k == KC - 1))
                    mm.then_inc(s["pj"], 1)

            def attention(a, b, n):
                s = at[a.name]
                sums = sums_psum(a)
                U, CH = a.units, a.chunk_at[-1]
                nw = 48 if a.bias else 16
                done = s["cp"] if a.topk else s["e"]
                U2 = a.seconds(U)

                def free(q, it):
                    if q < 0:
                        pe.wait_ge(s["te"], it * U)
                        pe.wait_ge(s["te2"], it * U2)
                        if not a.narrow:
                            pe.wait_ge(s["o"], it)
                        return
                    u = next(u for u in range(U) if a.chunk_at[u + 1] > q)
                    if q == a.chunk_at[u]:
                        pe.wait_ge(s["te"], it * U + u + 1)
                    else:
                        pe.wait_ge(s["te2"], it * U2 + a.seconds(u + 1))

                def turn(u, it):
                    i, j = a.unit(u)
                    pe.wait_ge(s["p"] if a.topk else s["e"], it * U + u + 1)
                    for c in range(a.chunks[u]):
                        q = a.chunk_at[u] + c
                        free(q - 2, it)
                        for kb in range(4 * c, min(4 * c + 4, i + 1)):
                            mm = pe.transpose(pT[q % 2][:, kb % 4 * P:kb % 4 * P + P],
                                              pr[:, u % 4, kb * P:kb * P + P], ident[:, :])
                        mm.then_inc(s["t"], 1)

                def values(p, it, halves=(0, 1)):
                    i, j = a.unit(2 * p)
                    mid = (i + 1) // 2
                    pe.wait_ge(s["te"], it * U + 2 * p + 2)
                    if a.seconds(2 * p + 2):
                        pe.wait_ge(s["te2"], it * U2 + a.seconds(2 * p + 2))
                    if p == 0:
                        pe.wait_ge(s["o"], it)
                        if a.narrow:
                            pe.wait_ge(s["vg"], it + 1)
                    for kb in range(0 if 0 in halves else mid, i + 1 if 1 in halves else mid):
                        for u in (2 * p, 2 * p + 1):
                            j = a.unit(u)[1]
                            sl = slice(j * a.slot, (j + 1) * a.slot)
                            mm = pe.matmul(pO[sl, i * P:i * P + P], vs[:, kb, sl],
                                           prT[:, u % 4, kb * P:kb * P + P],
                                           start=(kb == 0), stop=(kb == i))
                    if 1 in halves:
                        mm.then_inc(s["pv"], 1)

                def broadcast(it):
                    pe.wait_ge(s["te"], it * U + U)
                    pe.wait_ge(s["te2"], it * U2 + U2)
                    pe.wait_ge(s["ri"], it + 1)
                    for i in range(NT):
                        for j in range(a.hg):
                            sl = slice(j * a.slot, (j + 1) * a.slot)
                            u = a.unit_of(i, j)
                            mm = pe.matmul(sums[i // 4][sl, i % 4 * P:i % 4 * P + P],
                                           rinv[:, u:u + 1].to_broadcast([P, a.slot]), ident[:, :],
                                           start=True, stop=True)
                    mm.then_inc(s["bc"], 1)

                def tail_turns(it):
                    if a.topk:
                        turn(U - 2, it)
                        turn(U - 1, it)
                        values(a.pairs - 2, it)

                def tail_end(it):
                    values(a.pairs - 1, it)
                    broadcast(it)

                def group(g, it, first):
                    if first and a.narrow:
                        pe.wait_ge(s["vn"], b * 4 + 4)
                        pe.wait_ge(s["st"], (b + 1) * 16 * 2 * KC * len(TERMS))
                    elif first:
                        pe.wait_ge(ln[n]["ev"], b * 4 + 4)
                    if not a.narrow:
                        pe.wait_ge(done, it * U)
                        pe.wait_ge(s["w"], it * nw + nw)
                        for w in range(2):
                            for h in range(2):
                                for k in range(KC):
                                    mm = pe.matmul(pA[w][:, h * 512:h * 512 + 512], wq[:, k, w * P:w * P + P],
                                                   hT[:, k, h * 512:h * 512 + 512],
                                                   start=(k == 0), stop=(k == KC - 1))
                            mm.then_inc(s["pj"], 1)
                        if not first:
                            tail_turns(it - 1)
                            tail_end(it - 1)
                        pe.wait_ge(s["eqk"], it * (a.hg + 1) + a.hg)
                        for t in range(NT):
                            for k in range(KC):
                                mm = pe.matmul(pA[0][:, t * P:t * P + P], hT[:, k, t * P:t * P + P],
                                               wq[:, k, 2 * P:3 * P], start=(k == 0), stop=(k == KC - 1))
                        mm.then_inc(s["pj"], 1)
                        pe.wait_ge(s["eqk"], it * (a.hg + 1) + a.hg + 1)

                    def scores(u):
                        i, j = a.unit(u)
                        pe.wait_ge(done, it * U + a.units_before(u, 2, first or not a.narrow))
                        w = (i + 1) * P
                        for lo in range(0, w, 512):
                            hi = min(lo + 512, w)
                            if a.narrow:
                                h = g * a.hg + j
                                q = stack[0:KROWS, 0, bass.ds(h, 1), i * P:i * P + P].rearrange("p a n -> p (a n)")
                                k = stack[0:KROWS, 1, bass.ds(h, 1), lo:hi].rearrange("p a n -> p (a n)")
                            else:
                                q, k = qm[:, j, i * P:i * P + P], kT[:, lo:hi]
                            mm = pe.matmul(pA[(u + a.even) % 2][:, lo:hi], q, k, start=True, stop=(hi < w))
                        mm = pe.matmul(pA[(u + a.even) % 2][:, w - P:w], identm[:, :], tri[:, a.mask, :],
                                       start=False, stop=True)
                        mm.then_inc(s["s"], 1)

                    for u in range(2):
                        if u and not a.narrow:
                            pe.wait_ge(s["ev"], it + 1)
                        scores(u)
                    if a.narrow and not a.topk and not first:
                        tail_turns(it - 1)
                        tail_end(it - 1)
                    for p in range(a.pairs):
                        for u in (2 * p, 2 * p + 1):
                            if u + 2 < U:
                                scores(u + 2)
                            if not a.topk:
                                turn(u, it)
                                if p:
                                    values(p - 1, it, (u % 2,))
                        if a.topk:
                            if p == 0 and not first:
                                tail_turns(it - 1)
                            if p == 1 and not first:
                                tail_end(it - 1)
                            if p >= 1:
                                turn(2 * p - 2, it)
                                turn(2 * p - 1, it)
                            if p >= 2:
                                values(p - 2, it)

                def tail(g, it):
                    tail_turns(it)
                    tail_end(it)

                if a.narrow:
                    project_narrow(a, b, n)
                a.each_group(pe, b, group, tail)
                pe.wait_ge(s["o"], b * a.groups + a.groups)
                pe.wait_ge(s["wo"], b * 16 + 16)
                pe.wait_ge(s["te"], (b * a.groups + a.groups) * U)
                pe.wait_ge(s["te2"], (b * a.groups + a.groups) * a.seconds(U))
                oall = oall_n if a.narrow else oall_w
                for t in range(NT):
                    if t >= 2:
                        pe.wait_ge(s["x"], b * NT + t - 1)
                    for g in range(a.groups):
                        mm = pe.matmul(pT[t % 2][:, 0:D], oall[:, g, t * P:t * P + P], wo_sb[:, g, :],
                                       start=(g == 0), stop=(g == a.groups - 1))
                    mm.then_inc(s["y"], 1)

            with pe.Fori(0, B) as b:
                pe.wait_ge(s_bld, b * 128 + 128)
                pe.transpose(pT[0][:, 0:P], fmr[:, :], ident[:, :]).then_inc(s_fmt, 1)
                pe.wait_ge(s_fm, b + 1)
                norm("n0", b)
                attention(A0, b, "n0")
                norm("n1", b)
                pe.wait_ge(ln["n1"]["ev"], b * 4 + 4)
                for t in range(NT):
                    if t >= 2:
                        pe.wait_ge(f0["le"], b * NT + t - 1)
                    for k in range(KC):
                        mm = pe.matmul(pT[t % 2][:, 0:D], hT[:, k, t * P:t * P + P], wg[:, k, :],
                                       start=(k == 0), stop=(k == KC - 1))
                    mm.then_inc(f0["lg"], 1)
                pe.wait_ge(f0["w"], b * 16 + 16)

                def experts(t):
                    for half in range(2):
                        if t >= 1:
                            pe.wait_ge(f0["yc"], b * 2 * NT + 2 * t + half - 1)
                        for e2 in range(2):
                            e = 4 * half + 2 * e2
                            for k in range(KC):
                                mm = pe.matmul(pA[half][:, e2 * 512:e2 * 512 + 512], hT[:, k, t * P:t * P + P],
                                               we[:, k, e:e + 2, :], start=(k == 0), stop=(k == KC - 1))
                        mm.then_inc(f0["y"], 1)

                experts(0)
                pe.wait_ge(f0["g"], b + 1)
                for t in range(NT):
                    mm = pe.transpose(pT[t // 4][0:E, t % 4 * P:t % 4 * P + P], gate[:, t, :], ident[:, :])
                mm.then_inc(f0["gt"], 1)
                pe.wait_ge(f0["ge"], b * 2 + 2)
                for t in range(NT):
                    if t >= 2:
                        pe.wait_ge(f0["x"], b * NT + t - 1)
                    pe.matmul(pT[t % 2][:, 0:D], gT[:, t * P:t * P + P], be[:, :], start=True, stop=True)\
                      .then_inc(f0["yb"], 1)
                    if t:
                        experts(t)
                norm("n2", b)
                attention(A1, b, "n2")
                norm("n4", b)
                attention(A2, b, "n4")
                norm("n5", b)
                pe.wait_ge(ln["n5"]["ev"], b * 4 + 4)
                for t in range(NT):
                    for k in range(KC):
                        mm = pe.matmul(pT[0][:, t * E:t * E + E], hT[:, k, t * P:t * P + P], rw[:, k, :],
                                       start=(k == 0), stop=(k == KC - 1))
                mm.then_inc(m1["lg"], 1)
                with pe.Fori(0, E // 2) as ep:
                    it = b * (E // 2) + ep

                    def hidden(r):
                        par, half = r // 2, r % 2
                        if half == 0:
                            pe.wait_ge(m1["w%d" % par], it * 32 + 32)
                        for f in range(FC):
                            q = r * FC + f
                            pe.wait_ge(m1["ge"], it * 4 * FC + max(q - 3, 0))
                            for k in range(KC):
                                mm = pe.matmul(pA[q // 2 % 2][:, q % 2 * 512:q % 2 * 512 + 512],
                                               w1_sb[par][:, k, f * P:f * P + P],
                                               hT[:, k, half * 512:half * 512 + 512],
                                               start=(k == 0), stop=(k == KC - 1))
                            mm.then_inc(m1["h"], 1)

                    def down(r):
                        par, half = r // 2, r % 2
                        if r == 0:
                            pe.wait_ge(m1["df"], b + 1)
                        pe.wait_ge(m1["ge"], it * 4 * FC + (r + 1) * FC)
                        for t in range(4):
                            q = r * 4 + t
                            pe.wait_ge(m1["z"], it * 2 * NT + max(q - 1, 0))
                            for f in range(FC):
                                mm = pe.matmul(pT[q % 2][:, 0:D], H[half][:, f, t * P:t * P + P],
                                               w2_sb[par][:, f, :], start=(f == 0), stop=(f == FC - 1))
                            mm.then_inc(m1["y"], 1)

                    hidden(0)
                    for r in range(1, 4):
                        hidden(r)
                        down(r - 1)
                    down(3)

        @block.vector
        def _(v):
            ch = Chain(v, dv)
            v.wait_ge(s_cexp, 1)
            n = ch.mark(v.tensor_scalar(csig[:, :, :, :], csig[:, :, :, :], 1.0, None, ALU.add))
            ch.need(n)
            n = ch.mark(v.reciprocal(csig[:, :, :, :], csig[:, :, :, :]))
            ch.need(n)
            v.tensor_tensor(csig[:, :, :, :], csig[:, :, :, :], ctile[:, :, :, :], ALU.mult).then_inc(s_csil, 1)
            for l in range(2):
                v.wait_ge(s_mmm, l + 1)
                if l:
                    v.wait_ge(s_mst, 16)
                ch.mark(v.tensor_copy(modrow[:, 0:N], pA[0][0:B, :]))
                n = ch.mark(v.tensor_copy(modrow[:, N:6 * D], pA[1][0:B, 0:512]))
                ch.need(n)
                for j in (1, 4):
                    ch.mark(v.tensor_scalar(modrow[:, j * D:j * D + D], modrow[:, j * D:j * D + D], 1.0, None,
                                            ALU.add))
                for j in (2, 5):
                    r = modrow[:, j * D:j * D + D]
                    ch.mark(v.scalar_tensor_tensor(out=modtmp, in0=r, scalar=-1.0, in1=r, op0=ALU.mult,
                                                   op1=ALU.max))
                    n = ch.mark(v.tensor_scalar(modsgn, r, 0.0, 2.0, ALU.is_ge, ALU.mult))
                    ch.need(n)
                    n = ch.mark(v.tensor_scalar(modtmp, modtmp, 0.25, None, ALU.max))
                    ch.need(n)
                    n = ch.mark(v.scalar_tensor_tensor(out=r, in0=modsgn, scalar=-1.0, in1=modtmp, op0=ALU.add,
                                                       op1=ALU.mult))
                    ch.need(n)
                v.sem_inc(s_mrow, 1)
            ch.restart()
            v.wait_ge(s_wld, N_WLD)
            v.wait_ge(s_const, N_CONST)

            def stats(t, src):
                ch.need(ch.mark(v.bn_stats(st[:, t, :], src[:, t, :])))
                ch.mark(v.bn_aggr(mv[:, t, :], st[:, t, :]))

            def variance(n, h):
                ch.need(ch.n)
                v.tensor_scalar(ve[:, 4 * h:4 * h + 4], mv[:, 4 * h:4 * h + 4, 1], EPS, None, ALU.add)\
                 .then_inc(ln[n]["var"], 1)

            def normal(n, b, src, h):
                v.wait_ge(ln[n]["rs"], b * 2 + h + 1)
                for t in range(4 * h, 4 * h + 4):
                    v.tensor_scalar(xn[:, t, :], src[:, t, :], mv[:, t, 0:1], rstd[:, t:t + 1],
                                    ALU.subtract, ALU.mult).then_inc(ln[n]["xn"], 1)

            def norm(n, b, src):
                for h in range(2):
                    at0 = ch.n
                    for t in range(4):
                        ch.mark(v.bn_stats(st[:, 4 * h + t, :], src[:, 4 * h + t, :]))
                    for t in range(4):
                        ch.need(at0 + t + 1)
                        ch.mark(v.bn_aggr(mv[:, 4 * h + t, :], st[:, 4 * h + t, :]))
                    variance(n, h)
                for h in range(2):
                    normal(n, b, src, h)

            def norm_on_the_way(n, t, added, b, src):
                if t:
                    v.wait_ge(added, b * NT + t)
                    stats(t - 1, src)
                    if t == 4:
                        variance(n, 0)

            def norm_end(n, added, b, src):
                normal(n, b, src, 0)
                v.wait_ge(added, b * NT + NT)
                stats(NT - 1, src)
                variance(n, 1)
                normal(n, b, src, 1)

            def attention(a, b):
                s = at[a.name]
                U, CH = a.units, a.chunk_at[-1]
                nw = 48 if a.bias else 16
                if a.narrow:
                    for c in range(KC):
                        for x in range(2):
                            q = 2 * c + x
                            v.wait_ge(s["hn"], b * 8 + 4 * c + x + 1)
                            v.tensor_tensor(full[:, q, :], full[:, q, :], part[:, 4 * c + 2 * x, :], ALU.subtract)\
                             .then_inc(s["rn"], 1)
                        for x in range(2):
                            q = 2 * c + x
                            v.wait_ge(s["hn"], b * 8 + 4 * c + x + 3)
                            v.tensor_tensor(lowp[:, q, :], full[:, q, :], part[:, 4 * c + 2 * x + 1, :],
                                            ALU.subtract).then_inc(s["rn"], 1)
                    for t2 in range(4):
                        v.wait_ge(s["pj"], b * NT + 2 * t2 + 2)
                        psv = pA[t2 % 2][:, :].rearrange("p (t g d) -> p g t d", t=2, d=P)
                        if a.bias:
                            v.tensor_tensor(vall[:, :, 2 * t2:2 * t2 + 2, :], psv,
                                            bv_n[:, :].rearrange("p (g d) -> p g d", d=P).unsqueeze(2)
                                            .to_broadcast([P, 4, 2, P]), ALU.add)\
                             .then_inc(s["vn"], 1)
                        else:
                            v.tensor_copy(vall[:, :, 2 * t2:2 * t2 + 2, :], psv).then_inc(s["vn"], 1)
                ch.restart()
                oall = oall_n if a.narrow else oall_w

                def inverse(it):
                    v.wait_ge(s["rs"] if a.topk else s["e"], it * U + U)
                    v.reciprocal(rinv[:, 0:U], rsum[:, 0:U]).then_inc(s["ri"], 1)

                def normalise(g, it):
                    v.wait_ge(s["pv"], it * a.pairs + a.pairs)
                    v.wait_ge(s["be"], it * 2 + 2)
                    v.tensor_tensor(oall[:, bass.ds(g, 1), :].rearrange("p a n -> p (a n)"), pO[:, :], rbc[:, :],
                                    ALU.mult).then_inc(s["o"], 1)

                def tail(g, it):
                    inverse(it)
                    normalise(g, it)

                def group(g, it, first):
                    def select(p):
                        us = (2 * p, 2 * p + 1)
                        i = a.unit(us[0])[0]
                        w = (i + 1) * P
                        last = {}
                        if p:
                            ch.need(ch.n)
                        v.wait_ge(s["k"], it * U + a.units_before(us[0], 3, first))
                        v.wait_ge(s["cp"], it * U + us[0] + 2)
                        ch.mark(v.memset(step[:, :], 0.0))
                        for u in us:
                            last[u] = ch.mark(v.max(vals[:, u % 4, 0:8], ssb[:, u % 4, 0:w]))
                        ch.need(last[us[1]])
                        v.wait_ge(s["e"], it * U + a.units_before(us[0], 3, first))
                        c = us[0] % 4
                        v.tensor_scalar(nmax[:, c:c + 2], vals[:, c:c + 2, 0], -1.0, None, ALU.mult)\
                         .then_inc(s["mx"], 1)
                        for r in range(TOPK // 8 - 1):
                            for u in us:
                                ch.need(last[u])
                                src = ssb[:, u % 4, 0:w] if r == 0 else work[:, u % 2, 0:w]
                                last[u] = ch.mark(v.match_replace(
                                    out=work[:, u % 2, 0:w], in_to_replace=vals[:, u % 4, 8 * r:8 * r + 8],
                                    in_values=src, imm_value=NEG_REPLACED))
                            for u in us:
                                ch.need(last[u])
                                m = v.max(vals[:, u % 4, 8 * r + 8:8 * r + 16], work[:, u % 2, 0:w])
                                if r < TOPK // 8 - 2:
                                    last[u] = ch.mark(m)
                                else:
                                    m.then_inc(s["th"], 1)

                    def rowmax(u):
                        w = (a.unit(u)[0] + 1) * P
                        v.wait_ge(s["s"], it * U + u + 1)
                        v.wait_ge(s["e"], it * U + a.units_before(u, 4, first))
                        v.tensor_reduce(nmax[:, u % 4:u % 4 + 1], pA[(u + a.even) % 2][:, 0:w], AX, ALU.max,
                                        negate=True).then_inc(s["mx"], 1)

                    def out_of_psum(u):
                        w = min(a.unit(u)[0] + 1, 4) * P
                        q = a.chunk_at[u]
                        v.wait_ge(s["t"], it * CH + q + 1)
                        v.wait_ge(s["pv"], it * a.pairs + (max(u // 2 - 1, 0) if first else u // 2 - 1))
                        v.tensor_copy(prT[:, u % 4, 0:w], pT[q % 2][:, 0:w]).then_inc(s["te"], 1)

                    if a.topk:
                        for p in range(a.pairs):
                            select(p)
                            if p == 1 and not first:
                                inverse(it - 1)
                            if p == 2 and not first:
                                normalise(g - 1, it - 1)
                        ch.restart()
                        return
                    if not a.narrow:
                        if not first:
                            tail(g - 1, it - 1)
                        v.wait_ge(s["w"], it * nw + nw)
                        v.wait_ge(s["pj"], it * 3 + 3)
                        psv = pA[0][:, :].rearrange("p (t n) -> p t n", n=P)
                        v.tensor_tensor(vs[:, :, :], psv, bv_bc[:, :].unsqueeze(1).to_broadcast([P, NT, P]),
                                        ALU.add).then_inc(s["ev"], 1)
                    rowmax(0)
                    if a.narrow and not first:
                        inverse(it - 1)
                    rowmax(1)
                    for u in range(U):
                        if u + 2 < U:
                            rowmax(u + 2)
                        out_of_psum(u)
                        if u == 0 and a.narrow and not first:
                            normalise(g - 1, it - 1)

                a.each_group(v, b, group, tail)

            def project(a, b, dst, bias, gate_row, n_next):
                s = at[a.name]
                for t in range(NT):
                    norm_on_the_way(n_next, t, s["x"], b, dst)
                    v.wait_ge(s["y"], b * NT + t + 1)
                    y = pT[t % 2][:, 0:D]
                    if bias is not None:
                        n = ch.mark(v.tensor_tensor(tmp[t % 2], y, bias, ALU.add))
                        ch.need(n)
                        n = ch.mark(v.tensor_tensor(tmp[t % 2], tmp[t % 2], gate_row, ALU.mult))
                        ch.need(n)
                        y = tmp[t % 2]
                    v.tensor_tensor(dst[:, t, :], dst[:, t, :], y, ALU.add).then_inc(s["x"], 1)
                norm_end(n_next, s["x"], b, dst)

            with v.Fori(0, B) as b:
                v.wait_ge(s_bld, b * 128 + 128)
                norm("n0", b, X)
                attention(A0, b)
                project(A0, b, X, bo_bc[:, 0, :], bc[:, 0, :], "n1")
                for t in range(NT):
                    v.wait_ge(f0["lg"], b * NT + t + 1)
                    v.tensor_tensor(lg[:, t, :], pT[t % 2][:, 0:D], bg_bc[:, :], ALU.add).then_inc(f0["le"], 1)
                second = ch.n
                v.wait_ge(f0["le"], b * NT + NT)
                v.memset(ixf[:, :, :], 0.0)
                for t in range(NT):
                    ch.mark(v.max(v8[:, t, :], lg[:, t, :]))
                for t in range(NT):
                    ch.need(second + t + 1)
                    ch.mark(v.max_index(ix8[:, t, :], v8[:, t, :], lg[:, t, :]))
                ch.need(ch.n)
                v.tensor_scalar(gsm[:, :, 0], v8[:, :, 0], -1.0, None, ALU.mult).then_inc(f0["nm"], 1)
                n = ch.mark(v.tensor_scalar(ix8[:, :, 1], ix8[:, :, 0], E - 1, None, ALU.bitwise_and))
                ch.need(n)
                n = ch.mark(v.tensor_copy(ixf[:, :, 0], ix8[:, :, 1]))
                ch.need(n)
                iota_bc = iota8[:, :].unsqueeze(1).to_broadcast([P, NT, E])
                n = ch.mark(v.tensor_tensor(gate[:, :, :], iota_bc, ixf[:, :, 0:1].to_broadcast([P, NT, E]),
                                            ALU.is_equal))
                v.wait_ge(f0["se"], b * NT + NT)
                n = ch.mark(v.reciprocal(gsm[:, :, 2], gsm[:, :, 1]))
                ch.need(n)
                m = v.tensor_tensor(gate[:, :, :], gate[:, :, :], gsm[:, :, 2:3].to_broadcast([P, NT, E]), ALU.mult)
                m.then_inc(f0["g"], 1)
                v.wait_ge(f0["gt"], b + 1)
                for h in range(2):
                    v.tensor_copy(gT[:, h * 512:h * 512 + 512], pT[h][0:E, :]).then_inc(f0["ge"], 1)
                for t in range(NT):
                    norm_on_the_way("n2", t, f0["x"], b, X)
                    made = [0, 0]
                    for e in range(E):
                        c = e % 2
                        src = pA[e // 4][:, e % 4 * D:e % 4 * D + D]
                        if e % 4 == 0:
                            v.wait_ge(f0["y"], b * 2 * NT + 2 * t + e // 4 + 1)
                        if e < 2:
                            m = v.tensor_scalar(acc[c], src, gate[:, t, e:e + 1], None, ALU.mult)
                        else:
                            if made[c] is None:
                                v.wait_ge(f0["yc"], b * 2 * NT + 2 * t + 1)
                            else:
                                ch.need(made[c])
                            m = v.scalar_tensor_tensor(out=acc[c], in0=src, scalar=gate[:, t, e:e + 1],
                                                       in1=acc[c], op0=ALU.mult, op1=ALU.add)
                        if e % 4 == 3:
                            m.then_inc(f0["yc"], 1)
                            made[c] = None
                        else:
                            made[c] = ch.mark(m)
                    ch.need(made[0])
                    v.wait_ge(f0["yc"], b * 2 * NT + 2 * t + 2)
                    n = ch.mark(v.tensor_tensor(acc[2], acc[0], acc[1], ALU.add))
                    v.wait_ge(f0["yb"], b * NT + t + 1)
                    ch.need(n)
                    n = ch.mark(v.tensor_tensor(acc[3], acc[2], pT[t % 2][:, 0:D], ALU.add))
                    ch.need(n)
                    n = ch.mark(v.scalar_tensor_tensor(out=tmp[0], in0=acc[3], scalar=0.0, in1=bc[:, 1, :],
                                                       op0=ALU.max, op1=ALU.mult))
                    ch.need(n)
                    m = v.tensor_tensor(X[:, t, :], X[:, t, :], tmp[0], ALU.add)
                    m.then_inc(f0["x"], 1)
                norm_end("n2", f0["x"], b, X)
                attention(A1, b)
                project(A1, b, X, bo_bc[:, 1, :], bc[:, 2, :], "n3")
                v.wait_ge(ln["n3"]["xn"], b * NT + NT)
                for t in range(NT):
                    n = ch.mark(v.tensor_tensor(Z[:, t, :], xn[:, t, :], bc[:, 4, :], ALU.mult))
                ch.need(n)
                for t in range(NT):
                    n = ch.mark(v.tensor_tensor(Z[:, t, :], Z[:, t, :], bc[:, 3, :], ALU.add))
                ch.need(n)
                norm("n4", b, Z)
                attention(A2, b)
                project(A2, b, Z, None, None, "n5")
                v.wait_ge(m1["lg"], b + 1)
                n = ch.mark(v.tensor_copy(gate2[:, :, :], pT[0][:, 0:NT * E].rearrange("p (t e) -> p t e", e=E)))
                ch.need(n)
                for t in range(NT):
                    n = ch.mark(v.max(v8[:, t, :], gate2[:, t, :]))
                ch.need(n)
                v.tensor_tensor(gsm[:, :, 0], v8[:, :, 1], v8[:, :, 0], ALU.subtract).then_inc(m1["df"], 1)
                for t in range(NT):
                    n = ch.mark(v.max_index(ix8[:, t, :], v8[:, t, :], gate2[:, t, :]))
                ch.need(n)
                n = ch.mark(v.tensor_copy(ixf[:, :, :], ix8[:, :, 0:2]))
                v.wait_ge(m1["e1"], b + 1)
                n = ch.mark(v.tensor_scalar(gsm[:, :, 2], gsm[:, :, 1], 1.0, None, ALU.add))
                ch.need(n)
                n = ch.mark(v.reciprocal(gsm[:, :, 3], gsm[:, :, 2]))
                ch.need(n)
                n = ch.mark(v.tensor_tensor(gsm[:, :, 4], gsm[:, :, 1], gsm[:, :, 3], ALU.mult))
                for r, dst in ((0, gate), (1, gate2)):
                    n = ch.mark(v.tensor_tensor(dst[:, :, :], iota_bc, ixf[:, :, r:r + 1].to_broadcast([P, NT, E]),
                                                ALU.is_equal))
                ch.need(n)
                for r, dst in ((0, gate), (1, gate2)):
                    n = ch.mark(v.tensor_tensor(dst[:, :, :], dst[:, :, :],
                                                gsm[:, :, 3 + r:4 + r].to_broadcast([P, NT, E]), ALU.mult))
                ch.need(n)
                ch.mark(v.tensor_tensor(gate[:, :, :], gate[:, :, :], gate2[:, :, :], ALU.add))
                ch.restart()
                with v.Fori(0, E // 2) as ep:
                    it = b * (E // 2) + ep
                    for q in range(2 * NT):
                        par, t = q // NT, q % NT
                        v.wait_ge(m1["y"], it * 2 * NT + q + 1)
                        v.wait_ge(m1["z"], it * 2 * NT + max(q - NT + 1, 0))
                        v.scalar_tensor_tensor(out=Z[:, t, :], in0=pT[q % 2][:, 0:D],
                                               scalar=gate[:, t, bass.ds(ep * 2 + par, 1)], in1=Z[:, t, :],
                                               op0=ALU.mult, op1=ALU.add).then_inc(m1["z"], 1)
                v.wait_ge(m1["z"], b * E * NT + E * NT)
                for t in range(NT):
                    n = ch.mark(v.tensor_tensor(Z[:, t, :], Z[:, t, :], bc[:, 5, :], ALU.mult))
                ch.need(n)
                for t in range(NT):
                    n = ch.mark(v.tensor_tensor(X[:, t, :], X[:, t, :], Z[:, t, :], ALU.add))
                ch.need(n)
                v.sem_inc(s_fin, 1)
                ch.restart()


_INS = ["x", "ct", "wmod0", "wmod1", "wqkv0", "wqkv1", "wqkv2", "bqk0", "bqk1", "bv0", "bv1", "wo0", "wo1", "wo2",
        "bo0", "bo1", "ffn_wg", "ffn_bg", "ffn_we", "ffn_be", "ln_w", "router_w", "w1", "w2"]


def kernel(**inp):
    import numpy as np
    import concourse.bacc as _bacc
    from concourse.bass_utils import run_bass_kernel_spmd as _run

    def slots(w, slot):
        w = np.asarray(w)
        d = w.shape[-1] // 16
        w = w.reshape(w.shape[:-1] + (16, d))
        if d < slot:
            pad = np.zeros(w.shape[:-1] + (slot - d,), w.dtype)
            w = np.concatenate([w, pad], axis=-1)
        return w.reshape(w.shape[:-2] + (16 * slot // P, P))

    def group(wq, wk, wv, slot):
        ws = [slots(w, slot).reshape(KC, P, -1, P).transpose(2, 1, 0, 3) for w in (wq, wk, wv)]
        return np.ascontiguousarray(np.concatenate(ws, axis=3))

    def spread(w):
        w = np.asarray(w)
        return w.reshape(w.shape[:-1] + (KC, 8, 16)).swapaxes(-1, -2).reshape(w.shape)

    def narrow(wq, wk, wv):
        wq, wk = spread(wq), spread(wk)
        w = np.concatenate([wq, wk, slots(wv, 32).reshape(D, 4 * P)], axis=1)
        return np.ascontiguousarray(w.reshape(KC, P, N).transpose(1, 0, 2))

    def out_weights(w, slot):
        return np.ascontiguousarray(slots(np.asarray(w).T, slot).transpose(2, 1, 0))

    a = {k: np.asarray(v) for k, v in inp.items()}
    qkv = a["L1_attn_W_qkv"].reshape(D, 3, N)
    bqkv = a["L1_attn_b_qkv"].reshape(3, N)
    cat = a["L1_ffn_c_attn_w"].reshape(D, 3, D)
    arr = {
        "x": a["L0_attn_x"],
        "ct": np.ascontiguousarray(np.stack([a["L0_c"], a["L1_c"]]).reshape(2, B, KC, P).transpose(3, 0, 2, 1)),
        "wmod0": a["L0_wmod"], "wmod1": a["L1_wmod"],
        "wqkv0": narrow(a["L0_attn_Wq"].T, a["L0_attn_Wk"].T, a["L0_attn_Wv"].T),
        "wqkv1": group(qkv[:, 0], qkv[:, 1], qkv[:, 2], 64),
        "wqkv2": narrow(cat[:, 0], cat[:, 1], cat[:, 2]),
        "bqk0": np.ascontiguousarray(spread(np.stack([a["L0_attn_bq"], a["L0_attn_bk"]])).reshape(2, KC, P)
                                     .transpose(2, 0, 1)),
        "bqk1": np.ascontiguousarray(np.stack([slots(bqkv[0], 64), slots(bqkv[1], 64)], axis=2)),
        "bv0": np.ascontiguousarray(slots(a["L0_attn_bv"], 32).reshape(4 * P)),
        "bv1": np.ascontiguousarray(slots(bqkv[2], 64)),
        "wo0": out_weights(a["L0_attn_Wo"].T, 32),
        "wo1": out_weights(a["L1_attn_W_out"], 64),
        "wo2": out_weights(a["L1_ffn_c_proj_w"], 32),
        "bo0": a["L0_attn_bo"], "bo1": a["L1_attn_b_out"],
        "ffn_wg": a["L0_ffn_Wg"], "ffn_bg": a["L0_ffn_bg"], "ffn_be": a["L0_ffn_be"],
        "ffn_we": np.ascontiguousarray(a["L0_ffn_We"].reshape(E, KC, P, D).transpose(2, 1, 0, 3)),
        "ln_w": np.ascontiguousarray(np.stack([a["L1_ffn_ln1_w"], a["L1_ffn_ln2_w"]]).reshape(2, KC, P)
                                     .transpose(2, 0, 1)),
        "router_w": a["L1_ffn_router_w"],
        "w1": np.ascontiguousarray(a["L1_ffn_w1"].reshape(KC, P, E, F).transpose(2, 1, 0, 3)),
        "w2": np.ascontiguousarray(a["L1_ffn_w2"].reshape(E, FC, P, D).transpose(0, 2, 1, 3)),
    }
    nc = _bacc.Bacc("TRN2", target_bir_lowering=False, num_devices=1)
    ap, arrays = {}, {}
    for name in _INS:
        arrays[f"in_{name}"] = np.ascontiguousarray(arr[name])
        ap[name] = nc.dram_tensor(f"in_{name}", arr[name].shape, F32, kind="ExternalInput").ap()
    out = nc.dram_tensor("out_0", (B, N, D), F32, kind="ExternalOutput").ap()
    build(nc, ap["x"], ap["ct"], [ap["wmod0"], ap["wmod1"]], [ap["wqkv0"], ap["wqkv1"], ap["wqkv2"]],
          [ap["bqk0"], ap["bqk1"]], [ap["bv0"], ap["bv1"]], [ap["wo0"], ap["wo1"], ap["wo2"]],
          [ap["bo0"], ap["bo1"]], ap["ffn_wg"], ap["ffn_bg"], ap["ffn_we"], ap["ffn_be"], ap["ln_w"],
          ap["router_w"], ap["w1"], ap["w2"], out)
    r = _run(nc, [arrays], core_ids=[0])
    return r.results[0]["out_0"]
```
